# Optimizing a Trainium2 kernel written in Bass

```python
import numpy as np
import jax
import jax.numpy as jnp

def _softmax(x, axis=-1):
    return jax.nn.softmax(x, axis=axis)

def _gelu(x):
    return jax.nn.gelu(x, approximate=True)

def _silu(x):
    return jax.nn.silu(x)

def _sigmoid(x):
    return jax.nn.sigmoid(x)

def _layernorm(x, axis=-1, eps=1e-05):
    m = jnp.mean(x, axis=axis, keepdims=True)
    v = jnp.var(x, axis=axis, keepdims=True)
    return (x - m) / jnp.sqrt(v + eps)

def _scatter_add(tgt, idx, src, axis=0):
    return tgt.at[idx].add(src)

def _segment_sum(src, seg, n):
    return jax.ops.segment_sum(src, seg, n)
kernel_name = 'mk_recurrent_d2_jaxref_r8_621d87'

def setup_inputs(seed: int=0):
    np.random.seed(seed)
    _w = jnp.asarray

    def _L0_attn_setup():
        import jax, jax.numpy as jnp
        import numpy as np
        import math
        D_MODEL = 128
        NUM_HEADS = 16
        THETA = 10000.0

        def _rope(x, theta):
            n, d_k = (x.shape[-2], x.shape[-1])
            powers = jnp.arange(0, d_k, 2, dtype=jnp.float32) / d_k
            freqs = 1.0 / theta ** powers
            t = jnp.arange(n, dtype=jnp.float32)
            angles = jnp.outer(t, freqs)
            cos = jnp.cos(angles).astype(x.dtype)
            sin = jnp.sin(angles).astype(x.dtype)
            x_even = x[..., 0::2]
            x_odd = x[..., 1::2]
            rot_even = x_even * cos - x_odd * sin
            rot_odd = x_even * sin + x_odd * cos
            return jnp.stack([rot_even, rot_odd], axis=-1).reshape(x.shape)
        key = jax.random.key(seed)
        ks = jax.random.split(key, 5)
        B, N, D = (2, 256, D_MODEL)
        std = math.sqrt(2.0 / (D + D))
        x = jax.random.normal(ks[0], (B, N, D), dtype=jnp.float32)
        wq = jax.random.normal(ks[1], (D, D), dtype=jnp.float32) * std
        wk = jax.random.normal(ks[2], (D, D), dtype=jnp.float32) * std
        wv = jax.random.normal(ks[3], (D, D), dtype=jnp.float32) * std
        wo = jax.random.normal(ks[4], (D, D), dtype=jnp.float32) * std
        return {'x': x, 'wq': wq, 'wk': wk, 'wv': wv, 'wo': wo}
    _L0_attn_in = _L0_attn_setup()

    def _L0_ffn_setup():
        import jax, jax.numpy as jnp
        import numpy as np
        E = 8
        D = 128
        F = 512
        S, B = (256, 2)
        LN_EPS = 1e-05

        def _moe_forward(input_features, centroids, ln_g, ln_b, W1, b1, W2, b2):
            s, b, d = input_features.shape
            x = jnp.swapaxes(input_features, 0, 1).reshape(-1, d)
            logits = x.astype(jnp.float32) @ centroids.astype(jnp.float32).T
            assign = jnp.argmax(logits, axis=-1)
            onehot = jax.nn.one_hot(assign, E, dtype=x.dtype)
            disp = jnp.einsum('te,td->etd', onehot, x)
            mu = disp.mean(-1, keepdims=True)
            var = disp.var(-1, keepdims=True)
            xn = (disp - mu) * jax.lax.rsqrt(var + LN_EPS)
            xn = xn * ln_g[:, None, :] + ln_b[:, None, :]
            h = jax.nn.relu(jnp.einsum('etd,edf->etf', xn, W1) + b1[:, None, :])
            y = jnp.einsum('etf,efd->etd', h, W2) + b2[:, None, :]
            y = disp + y
            out = jnp.einsum('te,etd->td', onehot, y)
            return jnp.swapaxes(out.reshape(b, s, d), 0, 1)
        key = jax.random.key(seed)
        ks = jax.random.split(key, 8)
        scale_in = 1.0 / np.sqrt(D)
        scale_ff = 1.0 / np.sqrt(F)
        return {'input_features': jax.random.normal(ks[0], (S, B, D), dtype=jnp.float32), 'centroids': jax.random.normal(ks[1], (E, D), dtype=jnp.float32) * scale_in, 'ln_g': jnp.ones((E, D), dtype=jnp.float32), 'ln_b': jnp.zeros((E, D), dtype=jnp.float32), 'W1': jax.random.normal(ks[2], (E, D, F), dtype=jnp.float32) * scale_in, 'b1': jax.random.normal(ks[3], (E, F), dtype=jnp.float32) * 0.01, 'W2': jax.random.normal(ks[4], (E, F, D), dtype=jnp.float32) * scale_ff, 'b2': jax.random.normal(ks[5], (E, D), dtype=jnp.float32) * 0.01}
    _L0_ffn_in = _L0_ffn_setup()

    def _L1_attn_setup():
        import jax, jax.numpy as jnp
        import numpy as np
        NUM_HEADS = 16
        DIM = 128
        key = jax.random.key(seed)
        kx, kwq, kbq, kwk, kbk = jax.random.split(key, 5)
        B, N, C = (2, 256, DIM)
        s = 1.0 / np.sqrt(C)
        return {'x': jax.random.normal(kx, (B, N, C), dtype=jnp.float32), 'Wq': jax.random.normal(kwq, (C, C), dtype=jnp.float32) * s, 'bq': jax.random.normal(kbq, (C,), dtype=jnp.float32) * 0.01, 'Wk': jax.random.normal(kwk, (C, C), dtype=jnp.float32) * s, 'bk': jax.random.normal(kbk, (C,), dtype=jnp.float32) * 0.01}
    _L1_attn_in = _L1_attn_setup()

    def _L1_ffn_setup():
        import jax, jax.numpy as jnp
        import numpy as np
        B, S, D, H, E, K = (1, 512, 128, 512, 8, 2)

        def _ffn(x, w1, b1, w2, b2):
            h = jax.nn.gelu(x @ w1 + b1, approximate=False)
            return h @ w2 + b2
        key = jax.random.key(seed)
        ks = jax.random.split(key, 10)
        scale = 0.02
        return {'hidden_states': jax.random.normal(ks[0], (B, S, D), dtype=jnp.float32), 'gate_w': jax.random.normal(ks[1], (E, D), dtype=jnp.float32) * scale, 'w_in': jax.random.normal(ks[2], (E, D, H), dtype=jnp.float32) * scale, 'b_in': jnp.zeros((E, H), dtype=jnp.float32), 'w_out': jax.random.normal(ks[3], (E, H, D), dtype=jnp.float32) * scale, 'b_out': jnp.zeros((E, D), dtype=jnp.float32), 'sw_in': jax.random.normal(ks[4], (D, H), dtype=jnp.float32) * scale, 'sb_in': jnp.zeros((H,), dtype=jnp.float32), 'sw_out': jax.random.normal(ks[5], (H, D), dtype=jnp.float32) * scale, 'sb_out': jnp.zeros((D,), dtype=jnp.float32)}
    _L1_ffn_in = _L1_ffn_setup()
    _d = {'L0_attn_x': _L0_attn_in['x'], 'L0_attn_wq': _L0_attn_in['wq'], 'L0_attn_wk': _L0_attn_in['wk'], 'L0_attn_wv': _L0_attn_in['wv'], 'L0_attn_wo': _L0_attn_in['wo'], 'L0_ffn_centroids': _L0_ffn_in['centroids'], 'L0_ffn_ln_g': _L0_ffn_in['ln_g'], 'L0_ffn_ln_b': _L0_ffn_in['ln_b'], 'L0_ffn_W1': _L0_ffn_in['W1'], 'L0_ffn_b1': _L0_ffn_in['b1'], 'L0_ffn_W2': _L0_ffn_in['W2'], 'L0_ffn_b2': _L0_ffn_in['b2'], 'L1_attn_Wq': _L1_attn_in['Wq'], 'L1_attn_bq': _L1_attn_in['bq'], 'L1_attn_Wk': _L1_attn_in['Wk'], 'L1_attn_bk': _L1_attn_in['bk'], 'L1_ffn_gate_w': _L1_ffn_in['gate_w'], 'L1_ffn_w_in': _L1_ffn_in['w_in'], 'L1_ffn_b_in': _L1_ffn_in['b_in'], 'L1_ffn_w_out': _L1_ffn_in['w_out'], 'L1_ffn_b_out': _L1_ffn_in['b_out'], 'L1_ffn_sw_in': _L1_ffn_in['sw_in'], 'L1_ffn_sb_in': _L1_ffn_in['sb_in'], 'L1_ffn_sw_out': _L1_ffn_in['sw_out'], 'L1_ffn_sb_out': _L1_ffn_in['sb_out']}
    _x0 = _d['L0_attn_x']
    _d['L0_attn_x'] = jax.random.normal(jax.random.fold_in(jax.random.key(seed), 1), (8, 512, 128), dtype=_x0.dtype)
    del _x0
    return _d

def reference(L0_attn_x, L0_attn_wq, L0_attn_wk, L0_attn_wv, L0_attn_wo, L0_ffn_centroids, L0_ffn_ln_g, L0_ffn_ln_b, L0_ffn_W1, L0_ffn_b1, L0_ffn_W2, L0_ffn_b2, L1_attn_Wq, L1_attn_bq, L1_attn_Wk, L1_attn_bk, L1_ffn_gate_w, L1_ffn_w_in, L1_ffn_b_in, L1_ffn_w_out, L1_ffn_b_out, L1_ffn_sw_in, L1_ffn_sb_in, L1_ffn_sw_out, L1_ffn_sb_out):

    def _L0_attn_ref(x, wq, wk, wv, wo):
        import jax, jax.numpy as jnp
        import numpy as np
        import math
        D_MODEL = 128
        NUM_HEADS = 16
        THETA = 10000.0

        def _rope(x, theta):
            n, d_k = (x.shape[-2], x.shape[-1])
            powers = jnp.arange(0, d_k, 2, dtype=jnp.float32) / d_k
            freqs = 1.0 / theta ** powers
            t = jnp.arange(n, dtype=jnp.float32)
            angles = jnp.outer(t, freqs)
            cos = jnp.cos(angles).astype(x.dtype)
            sin = jnp.sin(angles).astype(x.dtype)
            x_even = x[..., 0::2]
            x_odd = x[..., 1::2]
            rot_even = x_even * cos - x_odd * sin
            rot_odd = x_even * sin + x_odd * cos
            return jnp.stack([rot_even, rot_odd], axis=-1).reshape(x.shape)
        B, N, D = x.shape
        H = NUM_HEADS
        d_k = D // H

        def split_heads(t):
            return t.reshape(B, N, H, d_k).transpose(0, 2, 1, 3)
        Q = split_heads(x @ wq.T)
        K = split_heads(x @ wk.T)
        V = split_heads(x @ wv.T)
        Q = _rope(Q, THETA)
        K = _rope(K, THETA)
        scale = 1.0 / math.sqrt(d_k)
        scores = jnp.einsum('bhqd,bhkd->bhqk', Q, K) * scale
        causal_mask = jnp.triu(jnp.ones((N, N), dtype=bool), k=1)
        scores = jnp.where(causal_mask, -jnp.inf, scores)
        attn = jax.nn.softmax(scores, axis=-1)
        out = jnp.einsum('bhqk,bhkd->bhqd', attn, V)
        out = out.transpose(0, 2, 1, 3).reshape(B, N, D)
        return out @ wo.T

    def _L0_ffn_ref(input_features, centroids, ln_g, ln_b, W1, b1, W2, b2):
        import jax, jax.numpy as jnp
        import numpy as np
        E = 8
        D = 128
        F = 512
        S, B = (256, 2)
        LN_EPS = 1e-05

        def _moe_forward(input_features, centroids, ln_g, ln_b, W1, b1, W2, b2):
            s, b, d = input_features.shape
            x = jnp.swapaxes(input_features, 0, 1).reshape(-1, d)
            logits = x.astype(jnp.float32) @ centroids.astype(jnp.float32).T
            assign = jnp.argmax(logits, axis=-1)
            onehot = jax.nn.one_hot(assign, E, dtype=x.dtype)
            disp = jnp.einsum('te,td->etd', onehot, x)
            mu = disp.mean(-1, keepdims=True)
            var = disp.var(-1, keepdims=True)
            xn = (disp - mu) * jax.lax.rsqrt(var + LN_EPS)
            xn = xn * ln_g[:, None, :] + ln_b[:, None, :]
            h = jax.nn.relu(jnp.einsum('etd,edf->etf', xn, W1) + b1[:, None, :])
            y = jnp.einsum('etf,efd->etd', h, W2) + b2[:, None, :]
            y = disp + y
            out = jnp.einsum('te,etd->td', onehot, y)
            return jnp.swapaxes(out.reshape(b, s, d), 0, 1)
        return _moe_forward(input_features, centroids, ln_g, ln_b, W1, b1, W2, b2)

    def _L1_attn_ref(x, Wq, bq, Wk, bk):
        import jax, jax.numpy as jnp
        import numpy as np
        NUM_HEADS = 16
        DIM = 128
        B, N, C = x.shape
        H = NUM_HEADS
        Dh = C // H
        q = (x @ Wq + bq).reshape(B, N, H, Dh).transpose(0, 2, 1, 3)
        k = (x @ Wk + bk).reshape(B, N, H, Dh).transpose(0, 2, 1, 3)
        v = k
        scale = C ** (-0.5)
        attn = jnp.einsum('bhnd,bhmd->bhnm', q, k) * scale
        attn = jax.nn.softmax(attn, axis=-1)
        out = jnp.einsum('bhnm,bhmd->bhnd', attn, v)
        return out.transpose(0, 2, 1, 3).reshape(B, N, C)

    def _L1_ffn_ref(hidden_states, gate_w, w_in, b_in, w_out, b_out, sw_in, sb_in, sw_out, sb_out):
        import jax, jax.numpy as jnp
        import numpy as np
        B, S, D, H, E, K = (1, 512, 128, 512, 8, 2)

        def _ffn(x, w1, b1, w2, b2):
            h = jax.nn.gelu(x @ w1 + b1, approximate=False)
            return h @ w2 + b2
        orig_shape = hidden_states.shape
        d = orig_shape[-1]
        x = hidden_states.reshape(-1, d)
        T = x.shape[0]
        n_exp = gate_w.shape[0]
        scores = jax.nn.softmax(x @ gate_w.T, axis=-1)
        topk_w, topk_idx = jax.lax.top_k(scores, K)
        w_tok = jnp.zeros((T, n_exp), dtype=x.dtype).at[jnp.arange(T)[:, None], topk_idx].add(topk_w)
        y = jnp.zeros_like(x)
        for e in range(n_exp):
            y = y + w_tok[:, e:e + 1] * _ffn(x, w_in[e], b_in[e], w_out[e], b_out[e])
        shared = _ffn(hidden_states, sw_in, sb_in, sw_out, sb_out)
        return y.reshape(orig_shape) + shared
    x = L0_attn_x
    xn = _layernorm(x, axis=-1)
    s = _L0_attn_ref(xn, L0_attn_wq, L0_attn_wk, L0_attn_wv, L0_attn_wo)
    g = _silu(_L0_ffn_ref(xn, L0_ffn_centroids, L0_ffn_ln_g, L0_ffn_ln_b, L0_ffn_W1, L0_ffn_b1, L0_ffn_W2, L0_ffn_b2))
    x = x + s * g
    xn = _layernorm(x, axis=-1)
    s = _L1_attn_ref(xn, L1_attn_Wq, L1_attn_bq, L1_attn_Wk, L1_attn_bk)
    g = _silu(_L1_ffn_ref(xn, L1_ffn_gate_w, L1_ffn_w_in, L1_ffn_b_in, L1_ffn_w_out, L1_ffn_b_out, L1_ffn_sw_in, L1_ffn_sb_in, L1_ffn_sw_out, L1_ffn_sb_out))
    x = x + s * g
    return x

_drawn_inputs = setup_inputs


def setup_inputs(seed=0):
    import zlib

    import numpy as np

    out = dict(_drawn_inputs(seed))
    spreads = {'L0_ffn_ln_g': (1.0, 0.6),
     'L0_ffn_ln_b': (0.0, 0.8),
     'L1_ffn_b_in': (0.0, 0.8),
     'L1_ffn_b_out': (0.0, 0.8),
     'L1_ffn_sb_in': (0.0, 0.8),
     'L1_ffn_sb_out': (0.0, 0.8)}
    factors = {'L0_ffn_b1': 8.0,
     'L0_ffn_b2': 8.0,
     'L1_attn_Wq': 8.0,
     'L1_attn_bq': 8.0,
     'L1_attn_Wk': 8.0,
     'L1_attn_bk': 64.0,
     'L1_ffn_gate_w': 8.0,
     'L1_ffn_w_in': 8.0,
     'L1_ffn_w_out': 8.0,
     'L1_ffn_sw_in': 8.0,
     'L1_ffn_sw_out': 8.0}
    for name, (base, spread) in spreads.items():
        noise = np.random.default_rng([zlib.crc32(name.encode()), seed]).standard_normal(out[name].shape)
        drawn = base * np.exp(spread * noise) if base else spread * noise
        out[name] = jnp.asarray(drawn.astype(out[name].dtype))
    for name, factor in factors.items():
        out[name] = (out[name] * factor).astype(out[name].dtype)
    return out
```

```python
from contextlib import ExitStack

import concourse.bass as bass
from concourse import mybir

F32 = mybir.dt.float32
BF16 = mybir.dt.bfloat16
U32 = mybir.dt.uint32
I32 = mybir.dt.int32
ALU = mybir.AluOpType
ACT = mybir.ActivationFunctionType
AX = mybir.AxisListType

P = 128
NB = 8
TB = 4
NT = NB * TB
H = 16
DH = 8
E = 8
F = 512
FC = F // P
G = 4
NG = H // G
VW = 32
KS = 48
KM = 50
EPS = 1e-5
BIG = 1e30
CHOICES = (1, 2)
SLOTS = (40, 72)
SCALE = (DH ** -0.5, P ** -0.5)
PARTS = ((0, 0, 1, 0, 2, 1), (0, 1, 0, 2, 0, 1))

C_ID, C_UP, C_ONE, C_MASK = 0, 128, 256, 384
C_DESC, C_J128, C_J, C_NHALF = 896, 904, 936, 1008
NCONST = 1012
W_1, W_2, W_B1, W_B2, W_G, W_LB = 0, F, 2 * F, 2 * F + FC, 2 * F + FC + P, 2 * F + FC + P + 1
NW = (2 * F + FC + P + 2, 2 * F + FC + P)


def wait(eng, sem, value):
    if isinstance(value, int) and value <= 0:
        return
    eng.wait_ge(sem, value)


def each(eng, n, body):
    body(0)
    with eng.Fori(1, n) as i:
        body(i)


def wait_apart(eng, sem, value, passed):
    eng.wait_ge(sem, value)
    if not isinstance(value, int):
        eng.sem_inc(passed, 1)


def build(nc, x_in, rope_in, const_in, w0_in, w1_in, e0_in, e1_in, out):
    ctx = ExitStack()
    with ctx:
        def sb(name, shape, dt=F32):
            return ctx.enter_context(nc.sbuf_tensor(name, shape, dt))

        def pb(name, shape, dt=F32):
            return ctx.enter_context(nc.psum_tensor(name, shape, dt))

        def sem(name):
            return ctx.enter_context(nc.semaphore(name))

        def dram(name, shape, dt):
            return nc.dram_tensor(name, shape, dt, kind="Internal").ap()

        epack = (e0_in, e1_in)
        qk_d = [dram(f"qk_d{L}", [2, NB, 6 * DH, H, TB * P], BF16) for L in (0, 1)]
        xs_d = [dram(f"xs_d{L}", [SLOTS[L] * P, P], F32) for L in (0, 1)]
        ys_d = [dram(f"ys_d{L}", [SLOTS[L] * P, P], F32) for L in (0, 1)]

        cst = sb("cst", [P, NCONST])
        rope = sb("rope", [P, 2, TB * P])
        w0 = sb("w0", [P, 6 * P + E])
        w1 = sb("w1", [P, 3 * P + E + 2 * F + 2 + P + FC + P])
        idb = cst[:, C_ID:C_ID + P]
        upb = sb("upb", [P, P], BF16)
        oneb = sb("oneb", [P, P], BF16)
        x_sb = sb("x_sb", [P, NT, P])
        xn_sb = sb("xn_sb", [P, NT, P])
        xs_sb = sb("xs_sb", [P, NT, P])
        v_sb = sb("v_sb", [P, NT, P])
        o_sb = sb("o_sb", [P, NT, P])
        yg_sb = sb("yg_sb", [P, NT, P])
        ptmp = yg_sb[:, :, :].rearrange("p a b -> p (a b)").rearrange("p (k s t) -> p k s t", k=4, s=2)
        cosq, sinq, qf, r1 = (ptmp[:, k] for k in range(4))
        parts = [sb(f"part{k}", [P, 2, TB * P], BF16) for k in range(3)]
        mv = sb("mv", [P, 2, TB, 2])
        st6 = sb("st6", [P, TB, 6])
        rstd = sb("rstd", [P, 2, TB])
        vare = sb("vare", [P, 2, TB])
        xns = sb("xns", [P, TB, P])
        xT = sb("xT", [P, TB * P])
        lg = sb("lg", [P, NT, E])
        Qs = sb("Qs", [64, NG, G, TB * P], BF16)
        Ks = sb("Ks", [64, NG, G, TB * P], BF16)
        PT = sb("PT", [P, 2, G, TB * P])
        hsh = PT[:, :, :, :]
        Vs = sb("Vs", [P, NG, TB, G, VW])
        mx = sb("mx", [P, NG, G, TB])
        mhi = sb("mhi", [G * TB, NG, P], BF16)
        mlo = sb("mlo", [G * TB, NG, P], BF16)
        dump = sb("dump", [P, 2, TB * P], BF16)
        oc = xT
        rec = sb("rec", [P, TB, G])
        big = PT[:, :, :, :].rearrange("p k h t -> p (k h) t")
        small = sb("small", [P, 8, 2 * NT])
        ohb = sb("ohb", [P, 2 * NT, E], BF16)
        pos = sb("pos", [P, 2 * NT], U32)
        tex = sb("tex", [P, SLOTS[1]], I32)
        wch = sb("wch", [P, 2, NT])
        zero = sb("zero", [P, P])
        we = sb("we", [P, 2, NW[0]])
        xe = sb("xe", [P, 2, P])
        xeT = sb("xeT", [P, 2, P])
        hb = parts[0][:, :, :].rearrange("p s t -> p (s t)").bitcast(F32).rearrange("p (c t) -> p c t", c=FC)
        hT = sb("hT", [P, 2, FC, P])
        ye = sb("ye", [P, 2, P])
        xn2s = hT[:, 0]

        ps = pb("ps", [P, 8, 512])

        s_load = sem("inputs_loaded")
        s_const = sem("constants_ready")
        s_setup = sem("setup_done")
        S = []
        LOADS = {n: sem(n) for n in "ld0 ld1 ld2 ld3 min0 min1 min2 min3 mT_ready mh_ready ml_ready".split()}
        BASE = (0, 32 * NB)
        for L in (0, 1):
            names = """chain_v chain_g chain_a x_stats rstd_ready xn_ready xn2_stats rstd2_ready xn2_ready xn_saved xT_psum xT_ready
                mm_q0 mm_q1 mm_v mm_lg rope_q0 rope_q1 qf_0 qf_1 p1_0 p1_1 r1_0 r1_1 p2_0 p2_1 p3_0 p3_1 out_0 out_1
                v_saved lg_saved rec_ready sh_psum sh_h sh_y sh_saved
                onehot_ready counts_ready pos_ready gate_exp zeroed scattered tiles_ready
                ld0 ld1 ld2 ld3 min0 min1 min2 min3 s_ready s_used mT_ready mh_ready ml_ready st_ready exp_done masked pv_done
                o_copied oT_done norm_done v_ready
                we0 we1 xe0 xe1 xeT_psum xeT_ready h_psum hb_ready h_ready mm2_done ye_ready yo0 yo1 gathered
                og oT2_psum oT2_ready s_psum z_ready silu_ready sg_ready x_ready""".split()
            unused = ("sh_psum sh_h sh_y sh_saved gate_exp", "xn2_stats rstd2_ready xn2_ready rope_q0 rope_q1 masked og oT2_psum oT2_ready s_psum")
            S.append({n: sem(f"{n}_{L}") for n in names if n not in unused[L].split() and n not in LOADS})
            S[L].update(LOADS)
        s_out = sem("out_stored")
        passed_dve = sem("passed_dve")
        passed_pool = passed_gpsimd = passed_dve
        block = ctx.enter_context(nc.Block())

        rows = lambda ap: ap.rearrange("(n p) d -> p n d", p=P)

        def mask_blocks(L, kt):
            return kt * P if L == 0 else 0

        @block.sync
        def _(sp):
            xr = x_in.rearrange("b (n p) d -> p (b n) d", p=P)
            for b in range(0, NT, 8):
                sp.dma_start(x_sb[:, b:b + 8, :], xr[:, b:b + 8, :]).then_inc(s_load, 16)
            sp.dma_start(cst[:, :], const_in).then_inc(s_load, 16)
            sp.dma_start(w0[:, :], w0_in).then_inc(s_load, 16)
            sp.dma_start(w1[:, :], w1_in).then_inc(s_load, 16)
            sp.dma_start(rope[:, :, :], rope_in).then_inc(s_load, 16)
            sp.wait_ge(s_setup, 2)
            for L in (0, 1):
                s = S[L]
                for j in range(0, SLOTS[L], 8):
                    sp.dma_start(rows(xs_d[L])[:, j:j + 8, :], zero[:, :].unsqueeze(1).broadcast_to([P, 8, P])).then_inc(s["zeroed"], 16)

                def step(b):
                    at = bass.ds(sp.snap(b * TB), TB)
                    sp.wait_ge(s["xn_ready"], TB * b + TB)
                    if L == 0:
                        sp.wait_ge(s["xn2_ready"], TB * b + TB)
                        sp.dma_start(xn_sb[:, at, :], xns[:, :, :]).then_inc(s["xn_saved"], 16)
                        sp.dma_start(xs_sb[:, at, :], xn2s[:, :, :]).then_inc(s["xn_saved"], 16)
                    else:
                        sp.dma_start(xs_sb[:, at, :], xns[:, :, :]).then_inc(s["xn_saved"], 16)
                    for i in (0, 1):
                        dst = qk_d[L][i, bass.ds(b, 1)].rearrange("o (c d) h t -> c (o d h) t", c=6)
                        for k in range(3):
                            sp.wait_ge(s[f"p{k + 1}_{i}"], b + 1)
                            for c in range(6):
                                if PARTS[i][c] == k:
                                    sp.dma_start(dst[c], parts[k][:, i, :]).then_inc(s[f"out_{i}"], 16)
                each(sp, NB, step)
                for i in (0, 1):
                    sp.wait_ge(s[f"out_{i}"], 16 * 6 * NB)

                def load(b, g):
                    wait(sp, s["exp_done"], 8 * (4 * b + g - 4) + 8)
                    bb = bass.ds(b, 1)
                    for dstk, i in ((Qs, 0), (Ks, 1)):
                        src = qk_d[L][i, bb, :, g * G:(g + 1) * G, :].rearrange("o r h t -> (o r) h t")
                        sp.dma_start(dstk[0:KS, g, :, :], src).then_inc(s[f"ld{g}"], 16)

                def maxima(b, g):
                    sp.wait_ge(s["ml_ready"], NB * NG * L + 4 * b + g + 1)
                    for r, m in ((KS, mhi), (KS + 1, mlo)):
                        dst = Qs[r:r + 1, g, :, :].rearrange("o h (q t) -> o (h q) t", t=P)
                        sp.dma_start(dst, m[:, g, :]).then_inc(s[f"min{g}"], 16)

                for g in range(NG):
                    load(0, g)
                maxima(0, 0)

                def slot(b, g, more, last):
                    if not last:
                        maxima(b + (g + 1) // NG, (g + 1) % NG)
                    if more:
                        load(b + 1, g)
                for g in range(NG):
                    slot(0, g, True, False)
                with sp.Fori(1, NB - 1) as b:
                    for g in range(NG):
                        slot(b, g, True, False)
                for g in range(NG):
                    slot(NB - 1, g, False, g == NG - 1)
                sp.wait_ge(s["tiles_ready"], 1)
                sp.wait_ge(s["scattered"], 16 * CHOICES[L] * NT)

                def feed(j, par):
                    wait(sp, s["mm2_done"], j - 1)
                    wait(sp, s["ye_ready"], j - 1)
                    e = sp.value_load(tex[0:1, bass.ds(j, 1)], min_val=0, max_val=E - 1)
                    sp.dma_start(we[:, par, 0:NW[L]], epack[L][bass.ds(e, 1), :, :].rearrange("o p n -> (o p) n")
                                 ).then_inc(s[f"we{par}"], 16)
                    sp.dma_start(xe[:, par, :], xs_d[L][bass.ds(j * P, P), :]).then_inc(s[f"xe{par}"], 16)

                def drain(j, par):
                    sp.wait_ge(s["ye_ready"], j + 1)
                    sp.dma_start(ys_d[L][bass.ds(j * P, P), :], ye[:, par, :]).then_inc(s[f"yo{par}"], 16)

                feed(0, 0)
                feed(1, 1)

                def step(jj):
                    for par in (0, 1):
                        feed(jj * 2 + par + 2, par)
                        drain(jj * 2 + par, par)
                each(sp, SLOTS[L] // 2 - 1, step)
                for par in (0, 1):
                    drain(SLOTS[L] - 2 + par, par)
                if L == 0:

                    def step(b):
                        sp.wait_ge(s["norm_done"], NB * NG)
                        wait(sp, s["oT2_psum"], b)
                        sp.dma_start(xns[:, :, :], o_sb[:, bass.ds(b * TB, TB), :]).then_inc(s["og"], 16)
                    each(sp, NB, step)
                else:
                    outr = out.rearrange("b (n p) d -> p (b n) d", p=P)
                    for b in range(NB):
                        sp.wait_ge(s["x_ready"], b + 1)
                        sp.dma_start(outr[:, b * TB:(b + 1) * TB, :], x_sb[:, b * TB:(b + 1) * TB, :]).then_inc(s_out, 16)
                    sp.wait_ge(s_out, 16 * NB)

        @block.gpsimd
        def _(pool):
            pool.memset(zero[:, :], 0.0).then_inc(s_setup, 1)
            pool.wait_ge(s_load, 16 * 8)
            for L in (0, 1):
                s = S[L]

                def rsqrt(b, k, stats, ready):
                    wait_apart(pool, s[stats], b + 1, passed_pool)
                    pool.tensor_scalar(vare[:, k, :], mv[:, k, :, 1], EPS, None, ALU.add).then_inc(s["chain_g"], 1)
                    pool.wait_ge(s["chain_g"], (b * (2 if L == 0 else 1) + k) + 1)
                    pool.tensor_tensor(rstd[:, k, :], vare[:, k, :], cst[:, C_NHALF:C_NHALF + TB], ALU.pow
                                       ).then_inc(s[ready], 1)

                def norm(b):
                    rsqrt(b, 0, "x_stats", "rstd_ready")
                    if L == 0:
                        rsqrt(b, 1, "xn2_stats", "rstd2_ready")

                def split(b):
                    for i in (0, 1):
                        if L == 0:
                            pool.wait_ge(s[f"rope_q{i}"], b + 1)
                            wait(pool, s[f"p3_{i}"], b)
                            wait(pool, s[f"r1_{i}"], b)
                            pool.tensor_tensor(qf[:, i, :], cosq[:, i, :], sinq[:, i, :], ALU.add
                                               ).then_inc(s[f"qf_{i}"], 1)
                    for i in (0, 1):
                        pool.wait_ge(s[f"p2_{i}"], b + 1)
                        wait(pool, s[f"out_{i}"], 16 * 6 * b)
                        pool.tensor_tensor(parts[2][:, i, :], r1[:, i, :], parts[1][:, i, :], ALU.subtract
                                           ).then_inc(s[f"p3_{i}"], 1)
                norm(0)

                def step(b):
                    norm(b + 1)
                    split(b)
                each(pool, NB - 1, step)
                split(NB - 1)
                pool.wait_ge(s["pos_ready"], 1)
                pool.wait_ge(s["zeroed"], 16 * SLOTS[L] // 8)
                pool.wait_ge(s["xn_saved"], 16 * NB * (2 if L == 0 else 1))

                def scatter(n):
                    pool.indirect_dma_start(xs_d[L], bass.IndirectOffsetOnAxis(ap=pos[:, n:n + 1], axis=0),
                                            xs_sb[:, n % NT, :], None).then_inc(s["scattered"], 16)

                def v_slot(b, g):
                    if not isinstance(b, int) or b:
                        wait_apart(pool, s["pv_done"], 4 * (4 * b + g - 4) + 4, passed_pool)
                    src = v_sb[:, bass.ds(b * TB, TB), g * G * DH:(g + 1) * G * DH].rearrange(
                        "p k (h d) -> p k h d", h=G)
                    pool.tensor_copy(Vs[:, g, :, :, 0:DH], src).then_inc(s["v_ready"], 1)

                def slot(b, g, more):
                    if more:
                        v_slot(b + (g + 2) // NG, (g + 2) % NG)
                    if L == 0:
                        for kt in range(TB):
                            for hp in (0, 1):
                                wait_apart(pool, s["exp_done"], 8 * (4 * b + g) + 2 * kt + hp + 1, passed_pool)
                                d = PT[:, kt % 2, 2 * hp:2 * hp + 2, kt * P:(kt + 1) * P]
                                pool.affine_select(out=d, in_=d, compare_op=ALU.is_ge, fill=0.0, base=0,
                                                   pattern=[[0, 2], [1, P]], channel_multiplier=-1
                                                   ).then_inc(s["masked"], 1)
                pool.wait_ge(s["v_saved"], NB)
                pool.wait_ge(s_setup, 2)
                v_slot(0, 0)
                v_slot(0, 1)
                for g in range(NG):
                    if L == 1:
                        for n in range(16 * g, 16 * g + 16):
                            scatter(n)
                    else:
                        for n in range(8 * g, 8 * g + 8):
                            scatter(n)
                    slot(0, g, True)
                with pool.Fori(1, NB - 1) as b:
                    for g in range(NG):
                        slot(b, g, True)
                for g in range(NG):
                    slot(NB - 1, g, g < 2)
                for par in (0, 1):
                    pool.wait_ge(s[f"yo{par}"], 16 * SLOTS[L] // 2)
                pool.wait_ge(s["pv_done"], 4 * NB * NG)
                for n in range(CHOICES[L] * NT):
                    dst = (yg_sb if n < NT else v_sb)[:, n % NT, :]
                    pool.indirect_dma_start(dst, None, ys_d[L],
                                            bass.IndirectOffsetOnAxis(ap=pos[:, n:n + 1], axis=0)
                                            ).then_inc(s["gathered"], 16)

        @block.scalar
        def _(act):
            act.wait_ge(s_load, 16 * 8)
            for L in (0, 1):
                s = S[L]

                def x_T(b):
                    act.wait_ge(s["xT_psum"], b + 1)
                    wait(act, s["mm_lg"] if L == 0 else s["sh_psum"], b if L == 0 else FC * b)
                    act.copy(xT[:, :], ps[:, 7, :]).then_inc(s["xT_ready"], 1)

                def post(b):
                    for i in (0, 1):
                        if L == 1:
                            act.wait_ge(s[f"mm_q{i}"], b + 1)
                            wait(act, s[f"p3_{i}"], b)
                            wait(act, s[f"r1_{i}"], b)
                            act.activation(qf[:, i, :], ps[:, 2 * i, :], ACT.Identity,
                                           bias=w1[:, 3 * P + E + 2 * F + i:3 * P + E + 2 * F + i + 1]
                                           ).then_inc(s[f"qf_{i}"], 1)
                    for i in (0, 1):
                        act.wait_ge(s[f"qf_{i}"], b + 1)
                        wait(act, s[f"out_{i}"], 16 * 6 * b)
                        act.copy(parts[0][:, i, :], qf[:, i, :]).then_inc(s[f"p1_{i}"], 1)
                    if L == 0:
                        act.wait_ge(s["mm_v"], b + 1)
                        act.copy(v_sb[:, bass.ds(b * TB, TB), :],
                                 ps[:, 4, :].rearrange("p (a c) -> p a c", a=TB)).then_inc(s["v_saved"], 1)
                    for i in (0, 1):
                        act.wait_ge(s[f"r1_{i}"], b + 1)
                        act.copy(parts[1][:, i, :], r1[:, i, :]).then_inc(s[f"p2_{i}"], 1)
                    if L == 1:
                        for c in range(FC):
                            act.wait_ge(s["sh_psum"], FC * b + c + 1)
                            wait(act, s["sh_y"], b)
                            act.activation(hsh[:, 0, c, :], ps[:, 1 if c % 2 == 0 else 3, :], ACT.Gelu,
                                           bias=w1[:, C_SBIN + c:C_SBIN + c + 1]).then_inc(s["sh_h"], 1)
                if L == 1:
                    C_SBIN = 3 * P + E + 2 * F + 2 + P
                x_T(0)

                def step(b):
                    post(b)
                    x_T(b + 1)
                each(act, NB - 1, step)
                post(NB - 1)
                if L == 1:
                    act.wait_ge(s["gate_exp"], 1)
                    act.activation(big[:, 1, 0:NT * E], big[:, 0, 0:NT * E], ACT.Exp).then_inc(s["gate_exp"], 1)
                    act.wait_ge(s["gate_exp"], 3)
                    act.activation(small[:, 2, 0:NT], small[:, 2, 0:NT], ACT.Exp).then_inc(s["gate_exp"], 1)

                def m_hi(b, g):
                    act.wait_ge(s["mT_ready"], NB * NG * L + 4 * b + g + 1)
                    wait(act, s[f"min{g}"], BASE[L] + 32 * b)
                    act.copy(mhi[:, g, :], ps[0:G * TB, 7, 0:P]).then_inc(s["mh_ready"], 1)

                def o_copy(b, g):
                    act.wait_ge(s["pv_done"], 4 * (4 * b + g) + 4)
                    wait(act, s["oT_done"], 4 * b + g)
                    act.copy(oc[:, :], ps[:, 6, :]).then_inc(s["o_copied"], 1)

                def prev(b, g):
                    return (b, g - 1) if g else (b - 1, NG - 1)

                def slot(b, g, last):
                    for kt in range(TB):
                        for hp in (0, 1):
                            u = 8 * (4 * b + g) + 2 * kt + hp
                            act.wait_ge(s["st_ready"], u + 1)
                            wait(act, s["pv_done"], 4 * (4 * b + g) + kt - 1)
                            q0 = mask_blocks(L, kt)
                            k = 2 * (u % 2 if isinstance(u, int) else hp)
                            act.activation(PT[:, kt % 2, 2 * hp:2 * hp + 2, q0:], ps[:, 2 * hp:2 * hp + 2, q0:],
                                           ACT.Exp, scale=SCALE[L]).then_inc(s["exp_done"], 1)
                            if (kt, hp) == (0, 1) and not (isinstance(b, int) and b == 0 and g == 0):
                                o_copy(*prev(b, g))
                            if (kt, hp) == (1, 0) and not last:
                                m_hi(b + (g + 1) // NG, (g + 1) % NG)
                m_hi(0, 0)
                for g in range(NG):
                    slot(0, g, False)
                with act.Fori(1, NB - 1) as b:
                    for g in range(NG):
                        slot(b, g, False)
                for g in range(NG):
                    slot(NB - 1, g, g == NG - 1)
                o_copy(NB - 1, NG - 1)


                def step(jj):
                    for par in (0, 1):
                        j = jj * 2 + par
                        act.wait_ge(s["hb_ready"], j + 1)
                        act.activation(hT[:, par].rearrange("p c t -> p (c t)"), hb[:, :, :].rearrange("p c t -> p (c t)"),
                                       ACT.Relu if L == 0 else ACT.Gelu).then_inc(s["h_ready"], 1)
                each(act, SLOTS[L] // 2, step)

                def step(b):
                    if L == 0:
                        act.wait_ge(s["oT2_psum"], b + 1)
                        wait(act, s["s_psum"], b)
                        act.copy(xT[:, :], ps[:, 7, :]).then_inc(s["oT2_ready"], 1)
                    act.wait_ge(s["z_ready"], b + 1)
                    wait(act, s["sg_ready"], b)
                    act.activation(r1[:, 0, :] if False else hT[:, 0:1].rearrange("p a c t -> p (a c t)"),
                                   hb[:, :, :].rearrange("p c t -> p (c t)"), ACT.Silu).then_inc(s["silu_ready"], 1)

                each(act, NB, step)
        @block.tensor
        def _(pe):
            pe.wait_ge(s_load, 16 * 8)
            pe.wait_ge(s_setup, 2)
            for L in (0, 1):
                s = S[L]
                if L == 1:
                    pe.wait_ge(S[0]["x_ready"], NB)

                def x_T(b):
                    pe.wait_ge(s["xn_ready"], TB * b + TB)
                    wait(pe, s["xT_ready"], b)
                    for n in range(TB):
                        mm = pe.transpose(ps[:, 7, n * P:(n + 1) * P], xns[:, n, :], idb)
                    mm.then_inc(s["xT_psum"], 1)

                def proj(b):
                    pe.wait_ge(s["xT_ready"], b + 1)
                    w = w0 if L == 0 else w1
                    for i in (0, 1):
                        if L == 0:
                            wait(pe, s[f"rope_q{i}"], b)
                            pe.matmul(ps[:, 2 * i, :], w[:, 2 * i * P:(2 * i + 1) * P], xT[:, :], start=True, stop=True)
                            mm = pe.matmul(ps[:, 2 * i + 1, :], w[:, (2 * i + 1) * P:(2 * i + 2) * P], xT[:, :],
                                           start=True, stop=True)
                        else:
                            wait(pe, s[f"qf_{i}"], b)
                            mm = pe.matmul(ps[:, 2 * i, :], w[:, i * P:(i + 1) * P], xT[:, :], start=True, stop=True)
                        mm.then_inc(s[f"mm_q{i}"], 1)
                    wait(pe, s["v_saved"], b)
                    wv = w0[:, 4 * P:5 * P] if L == 0 else w1[:, 2 * P:3 * P]
                    for n in range(TB):
                        mm = pe.matmul(ps[:, 4, n * P:(n + 1) * P], xT[:, n * P:(n + 1) * P], wv, start=True, stop=True)
                    mm.then_inc(s["mm_v"], 1)
                    wait(pe, s["lg_saved"], b)
                    wr = w0[:, 6 * P:6 * P + E] if L == 0 else w1[:, 3 * P:3 * P + E]
                    for n in range(TB):
                        mm = pe.matmul(ps[:, 5, n * E:(n + 1) * E], xT[:, n * P:(n + 1) * P], wr, start=True, stop=True)
                    mm.then_inc(s["mm_lg"], 1)
                    if L == 1:
                        sw = 3 * P + E
                        for c in range(FC):
                            wait(pe, s["sh_h"], FC * b + (c - 1 if c >= 2 else 0))
                            mm = pe.matmul(ps[:, 1 if c % 2 == 0 else 3, :], w1[:, sw + c * P:sw + (c + 1) * P], xT[:, :],
                                           start=True, stop=True)
                            mm.then_inc(s["sh_psum"], 1)

                def shared(b):
                    pe.wait_ge(s["sh_h"], FC * b + FC)
                    wait(pe, s["sh_saved"], b)
                    sw = 3 * P + E + F
                    for n in range(TB):
                        for c in range(FC):
                            mm = pe.matmul(ps[:, 6, n * P:(n + 1) * P], hsh[:, 0, c, n * P:(n + 1) * P],
                                           w1[:, sw + c * P:sw + (c + 1) * P], start=(c == 0), stop=(c == FC - 1))
                    mm.then_inc(s["sh_y"], 1)
                x_T(0)

                def step(b):
                    proj(b)
                    x_T(b + 1)
                    if L == 1:
                        shared(b)
                each(pe, NB - 1, step)
                proj(NB - 1)
                if L == 1:
                    shared(NB - 1)
                KT = CHOICES[L] * NT
                pe.wait_ge(s["onehot_ready"], 1)
                pe.matmul(ps[:, 0, 0:KT * E], upb[:, :], ohb[:, 0:KT, :].rearrange("p n e -> p (n e)"),
                          start=True, stop=True)
                pe.matmul(ps[:, 1, 0:KT * E], oneb[:, :], ohb[:, 0:KT, :].rearrange("p n e -> p (n e)"),
                          start=True, stop=True).then_inc(s["counts_ready"], 1)

                def first_pass(b, g, n):
                    h, qt = n // TB, n % TB
                    if n == 0:
                        pe.wait_ge(s[f"ld{g}"], BASE[L] + 32 * b + 32)
                    N = (qt + 1) * P if L == 0 else TB * P
                    wait(pe, s["s_used"], 16 * (4 * b + g) + n - 1)
                    pe.matmul(ps[:, 4 + n % 2, 0:N], Qs[0:KS, g, h, qt * P:(qt + 1) * P], Ks[0:KS, g, h, 0:N],
                              start=True, stop=True).then_inc(s["s_ready"], 1)

                def m_T(b, g):
                    pe.wait_ge(s["s_used"], 16 * (4 * b + g) + 16)
                    wait(pe, s["norm_done"], 4 * b + g - 2)
                    pe.transpose(ps[0:G * TB, 7, 0:P], mx[:, g].rearrange("p h q -> p (h q)"), idb
                                 ).then_inc(s["mT_ready"], 1)

                def o_T(b, g, last):
                    pe.wait_ge(s["o_copied"], 4 * b + g + 1)
                    if last:
                        pe.wait_ge(s["norm_done"], 4 * b + g)
                    else:
                        pe.wait_ge(s["ml_ready"], NB * NG * L + 4 * b + g + 3)
                    for n in range(TB):
                        mm = pe.transpose(ps[:, 7, n * P:(n + 1) * P], oc[:, n * P:(n + 1) * P], idb)
                    mm.then_inc(s["oT_done"], 1)

                def weighted_v(b, g, kt):
                    t = 4 * b + g
                    if L == 0:
                        pe.wait_ge(s["masked"], 8 * t + 2 * kt + 2)
                    else:
                        pe.wait_ge(s["exp_done"], 8 * t + 2 * kt + 2)
                    if kt == 0:
                        pe.wait_ge(s["v_ready"], t + 1)
                        wait(pe, s["o_copied"], t)
                    q0 = mask_blocks(L, kt)
                    for h in range(G):
                        mm = pe.matmul(ps[h * VW:(h + 1) * VW, 6, q0:], Vs[:, g, kt, h, :], PT[:, kt % 2, h, q0:],
                                       start=(kt == 0), stop=(kt == TB - 1), skip_group_check=True)
                    mm.then_inc(s["pv_done"], 1)

                def prev(b, g):
                    return (b, g - 1) if g else (b - 1, NG - 1)

                def slot(b, g, more, last):
                    first = isinstance(b, int) and b == 0 and g == 0
                    for kt in range(TB):
                        for hp in (0, 1):
                            u = 8 * (4 * b + g) + 2 * kt + hp
                            if kt == 0 and hp == 0:
                                pe.wait_ge(s[f"min{g}"], BASE[L] + 32 * b + 32)
                            wait(pe, s["exp_done"], u - 1)
                            q0 = mask_blocks(L, kt)
                            for h in (2 * hp, 2 * hp + 1):
                                mm = pe.matmul(ps[:, h, q0:], Ks[0:KM, g, h, kt * P:(kt + 1) * P], Qs[0:KM, g, h, q0:],
                                               start=True, stop=True)
                            mm.then_inc(s["st_ready"], 1)
                            if more:
                                for n in range(4 * kt + 2 * hp, 4 * kt + 2 * hp + 2):
                                    first_pass(b + (g + 2) // NG, (g + 2) % NG, n)
                            if hp == 1:
                                if kt:
                                    weighted_v(b, g, kt - 1)
                                elif not first:
                                    weighted_v(*prev(b, g), TB - 1)
                            if (kt, hp) == (1, 0) and not last:
                                m_T(b + (g + 1) // NG, (g + 1) % NG)
                            if (kt, hp) == (2, 0) and not first:
                                o_T(*prev(b, g), last)
                for g in (0, 1):
                    for n in range(16):
                        first_pass(0, g, n)
                m_T(0, 0)
                for g in range(NG):
                    slot(0, g, True, False)
                with pe.Fori(1, NB - 1) as b:
                    for g in range(NG):
                        slot(b, g, True, False)
                for g in range(NG):
                    slot(NB - 1, g, g < 2, g == NG - 1)
                weighted_v(NB - 1, NG - 1, TB - 1)
                pe.wait_ge(s["o_copied"], NB * NG)
                pe.wait_ge(s["norm_done"], NB * NG - 1)
                for n in range(TB):
                    mm = pe.transpose(ps[:, 7, n * P:(n + 1) * P], oc[:, n * P:(n + 1) * P], idb)
                mm.then_inc(s["oT_done"], 1)

                def up(j, par):
                    pe.wait_ge(s[f"xe{par}"], 16 * (j // 2 + 1) if isinstance(j, int) else 16 * (j[0] + 1))
                    jn = j if isinstance(j, int) else 2 * j[0] + par
                    wait(pe, s["xeT_ready"], jn)
                    pe.transpose(ps[:, 0, 0:P], xe[:, par, :], idb).then_inc(s["xeT_psum"], 1)
                    pe.wait_ge(s["xeT_ready"], jn + 1)
                    pe.wait_ge(s[f"we{par}"], 16 * (j // 2 + 1) if isinstance(j, int) else 16 * (j[0] + 1))
                    wait(pe, s["hb_ready"], jn)
                    for c in range(FC):
                        mm = pe.matmul(ps[:, 1, c * P:(c + 1) * P], we[:, par, W_1 + c * P:W_1 + (c + 1) * P],
                                       xeT[:, par, :], start=True, stop=True)
                    mm.then_inc(s["h_psum"], 1)

                def down(j, par):
                    jn = j if isinstance(j, int) else 2 * j[0] + par
                    pe.wait_ge(s["h_ready"], jn + 1)
                    wait(pe, s["ye_ready"], jn - 1 if isinstance(jn, int) else jn)
                    for c in range(FC):
                        mm = pe.matmul(ps[:, 2 + par, 0:P], hT[:, par, c, :], we[:, par, W_2 + c * P:W_2 + (c + 1) * P],
                                       start=(c == 0), stop=(c == FC - 1))
                    mm.then_inc(s["mm2_done"], 1)
                pe.wait_ge(s["norm_done"], NB * NG)
                up(0, 0)

                def step(jj):
                    up((jj,), 1)
                    down((jj,), 0)
                    up((jj + 1,), 0)
                    down((jj,), 1)
                each(pe, SLOTS[L] // 2 - 1, step)
                n = SLOTS[L] - 2
                up(n + 1, 1)
                down(n, 0)
                down(n + 1, 1)
                if L == 0:

                    def step(b):
                        pe.wait_ge(s["og"], 16 * b + 16)
                        wait(pe, s["oT2_ready"], b)
                        for n in range(TB):
                            mm = pe.transpose(ps[:, 7, n * P:(n + 1) * P], xns[:, n, :], idb)
                        mm.then_inc(s["oT2_psum"], 1)
                        pe.wait_ge(s["oT2_ready"], b + 1)
                        wait(pe, s["sg_ready"], b)
                        for n in range(TB):
                            mm = pe.matmul(ps[:, 6, n * P:(n + 1) * P], xT[:, n * P:(n + 1) * P], w0[:, 5 * P:6 * P],
                                           start=True, stop=True)
                        mm.then_inc(s["s_psum"], 1)

                    each(pe, NB, step)
        @block.vector
        def _(dve):
            dve.wait_ge(s_load, 16 * 8)
            dve.tensor_copy(upb[:, :], cst[:, C_UP:C_UP + P]).then_inc(s_const, 1)
            dve.tensor_copy(oneb[:, :], cst[:, C_ONE:C_ONE + P]).then_inc(s_const, 1)
            dve.memset(Qs[:, :, :, :], 0.0).then_inc(s_const, 1)
            dve.memset(Ks[:, :, :, :], -1.0).then_inc(s_const, 1)
            dve.memset(Vs[:, :, :, :, :], 0.0).then_inc(s_const, 1)
            dve.wait_ge(s_const, 5)
            dve.memset(Vs[:, :, :, :, DH:DH + 1].rearrange("p g k h o -> p (g k h) o"), 1.0).then_inc(s_setup, 1)
            for L in (0, 1):
                s = S[L]
                chained = [0]

                def chain(ins):
                    chained[0] += 1
                    ins.then_inc(s["chain_v"], 1)
                    dve.wait_ge(s["chain_v"], chained[0])

                def stats(b, k, src, ready, free, count):
                    for n in range(TB):
                        ins = dve.bn_stats(st6[:, n, :], src(n))
                        ins.then_inc(s[free], 1)
                    wait_apart(dve, s[free], count, passed_dve)
                    for n in range(TB):
                        ins = dve.bn_aggr(mv[:, k, n, :], st6[:, n, :])
                    ins.then_inc(s[ready], 1)

                def norm(b):
                    per = 2 * TB if L == 0 else TB
                    stats(b, 0, lambda n: x_sb[:, bass.ds(b * TB + n, 1), :].rearrange("p o d -> p (o d)"), "x_stats",
                          "chain_a", per * b + TB)
                    dve.wait_ge(s["rstd_ready"], b + 1)
                    wait(dve, s["xT_psum"], b)
                    wait(dve, s["xn_saved"], 16 * (2 if L == 0 else 1) * b)
                    for n in range(TB):
                        ins = dve.tensor_scalar(xns[:, n, :], x_sb[:, bass.ds(b * TB + n, 1), :].rearrange("p o d -> p (o d)"),
                                                mv[:, 0, n, 0:1], rstd[:, 0, n:n + 1], ALU.subtract, ALU.mult)
                        ins.then_inc(s["xn_ready"], 1)
                    if L == 0:
                        dve.wait_ge(s["xn_ready"], TB * b + TB)
                        stats(b, 1, lambda n: xns[:, n, :], "xn2_stats", "chain_a", per * b + 2 * TB)
                        dve.wait_ge(s["rstd2_ready"], b + 1)
                        for n in range(TB):
                            ins = dve.tensor_scalar(xn2s[:, n, :], xns[:, n, :], mv[:, 1, n, 0:1], rstd[:, 1, n:n + 1],
                                                    ALU.subtract, ALU.mult)
                            ins.then_inc(s["xn2_ready"], 1)

                def post(b):
                    for i in (0, 1):
                        if L == 0:
                            dve.wait_ge(s[f"mm_q{i}"], b + 1)
                            wait(dve, s[f"qf_{i}"], b)
                            dve.tensor_tensor(cosq[:, i, :], ps[:, 2 * i, :], rope[:, 0, :], ALU.mult)
                            dve.tensor_tensor(sinq[:, i, :], ps[:, 2 * i + 1, :], rope[:, 1, :], ALU.mult
                                              ).then_inc(s[f"rope_q{i}"], 1)
                    if L == 1:
                        dve.wait_ge(s["mm_v"], b + 1)
                        bk = w1[:, 3 * P + E + 2 * F + 2:3 * P + E + 2 * F + 2 + P].unsqueeze(1).broadcast_to([P, TB, P])
                        dve.tensor_tensor(v_sb[:, bass.ds(b * TB, TB), :], ps[:, 4, :].rearrange("p (a c) -> p a c", a=TB),
                                          bk, ALU.add).then_inc(s["v_saved"], 1)
                    dve.wait_ge(s["mm_lg"], b + 1)
                    dve.tensor_copy(lg[:, bass.ds(b * TB, TB), :], ps[:, 5, 0:TB * E].rearrange("p (a e) -> p a e", a=TB)
                                    ).then_inc(s["lg_saved"], 1)
                    for i in (0, 1):
                        dve.wait_ge(s[f"p1_{i}"], b + 1)
                        wait(dve, s[f"p3_{i}"], b)
                        wait(dve, s[f"p2_{i}"], b)
                        dve.tensor_tensor(r1[:, i, :], qf[:, i, :], parts[0][:, i, :], ALU.subtract
                                          ).then_inc(s[f"r1_{i}"], 1)
                    if L == 1:
                        dve.wait_ge(s["sh_y"], b + 1)
                        sbo = w1[:, 3 * P + E + 2 * F + 2 + P + FC:3 * P + E + 2 * F + 2 + P + FC + P].unsqueeze(1).broadcast_to([P, TB, P])
                        dve.tensor_tensor(xn_sb[:, bass.ds(b * TB, TB), :], ps[:, 6, :].rearrange("p (a c) -> p a c", a=TB),
                                          sbo, ALU.add).then_inc(s["sh_saved"], 1)
                norm(0)

                def step(b):
                    norm(b + 1)
                    post(b)
                each(dve, NB - 1, step)
                post(NB - 1)

                K = CHOICES[L]
                KT = K * NT
                dve.wait_ge(s["lg_saved"], NB)

                def v3(k, n=KT):
                    return big[:, k, 0:n * E].rearrange("p (n e) -> p n e", e=E)

                def bc(ap, n):
                    return ap.unsqueeze(2).broadcast_to([P, n, E])
                desc = cst[:, C_DESC:C_DESC + E].unsqueeze(1).broadcast_to([P, NT, E])
                src = lg[:, :, :]
                for k in range(K):
                    top = small[:, k, 0:NT]
                    chain(dve.tensor_reduce(top, src, AX.X, ALU.max))
                    chain(dve.tensor_tensor(v3(0, NT), src, bc(top, NT), ALU.is_equal))
                    chain(dve.tensor_tensor(v3(0, NT), v3(0, NT), desc, ALU.mult))
                    chain(dve.tensor_reduce(small[:, 2, 0:NT], v3(0, NT), AX.X, ALU.max))
                    chain(dve.tensor_tensor(ohb[:, k * NT:(k + 1) * NT, :], desc, bc(small[:, 2, 0:NT], NT), ALU.is_equal))
                    if k + 1 < K:
                        chain(dve.tensor_scalar(v3(1, NT), ohb[:, 0:NT, :], -BIG, None, ALU.mult))
                        chain(dve.tensor_tensor(v3(3, NT), lg[:, :, :], v3(1, NT), ALU.add))
                        src = v3(3, NT)
                dve.sem_inc(s["onehot_ready"], 1)
                if L == 1:
                    chain(dve.tensor_tensor(v3(0, NT), lg[:, :, :], bc(small[:, 0, 0:NT], NT), ALU.subtract))
                    dve.sem_inc(s["gate_exp"], 1)
                    dve.wait_ge(s["gate_exp"], 2)
                    chain(dve.tensor_reduce(small[:, 3, 0:NT], v3(1, NT), AX.X, ALU.add))
                    chain(dve.tensor_tensor(small[:, 2, 0:NT], small[:, 1, 0:NT], small[:, 0, 0:NT], ALU.subtract))
                    dve.sem_inc(s["gate_exp"], 1)
                    dve.wait_ge(s["gate_exp"], 4)
                    chain(dve.reciprocal(wch[:, 0, :], small[:, 3, 0:NT]))
                    chain(dve.tensor_tensor(wch[:, 1, :], small[:, 2, 0:NT], wch[:, 0, :], ALU.mult))
                dve.wait_ge(s["counts_ready"], 1)
                cnt = ps[:, 1, 0:KT * E].rearrange("p (n e) -> p n e", e=E)
                rank = ps[:, 0, 0:KT * E].rearrange("p (n e) -> p n e", e=E)
                chain(dve.tensor_copy(v3(0), cnt))
                a, d = 0, 1
                while d < KT:
                    chain(dve.tensor_copy(v3(1 - a)[:, 0:d, :], v3(a)[:, 0:d, :]))
                    chain(dve.tensor_tensor(v3(1 - a)[:, d:KT, :], v3(a)[:, d:KT, :], v3(a)[:, 0:KT - d, :], ALU.add))
                    a, d = 1 - a, 2 * d
                total = v3(a)[:, KT - 1, :]
                tile_of = big[:, 3, 0:E * NT].rearrange("p (e j) -> p e j", e=E)
                chain(dve.tensor_tensor(tile_of, total.unsqueeze(2).broadcast_to([P, E, NT]),
                                        cst[:, C_J128:C_J128 + NT].unsqueeze(1).broadcast_to([P, E, NT]), ALU.is_gt))
                chain(dve.tensor_reduce(small[:, 4, 0:E], tile_of, AX.X, ALU.add))
                chain(dve.tensor_copy(small[:, 5, 0:E], small[:, 4, 0:E]))
                c, d = 5, 1
                while d < E:
                    chain(dve.tensor_copy(small[:, 11 - c, 0:d], small[:, c, 0:d]))
                    chain(dve.tensor_tensor(small[:, 11 - c, d:E], small[:, c, d:E], small[:, c, 0:E - d], ALU.add))
                    c, d = 11 - c, 2 * d
                nj = SLOTS[L]
                te = big[:, 3, 0:nj * E].rearrange("p (j e) -> p j e", e=E) if nj * E <= 2 * NT * E else None
                half = nj // 2
                for q in (0, 1):
                    te = big[:, 3, 0:half * E].rearrange("p (j e) -> p j e", e=E)
                    js = cst[:, C_J + q * half:C_J + (q + 1) * half].unsqueeze(2).broadcast_to([P, half, E])
                    chain(dve.tensor_tensor(te, js, small[:, c, 0:E].unsqueeze(1).broadcast_to([P, half, E]), ALU.is_ge))
                    chain(dve.tensor_reduce(small[:, 7, 0:half], te, AX.X, ALU.add))
                    chain(dve.tensor_scalar(tex[:, q * half:(q + 1) * half], small[:, 7, 0:half], float(E - 1), None, ALU.min))
                dve.sem_inc(s["tiles_ready"], 1)
                chain(dve.tensor_tensor(small[:, 11 - c, 0:E], small[:, c, 0:E], small[:, 4, 0:E], ALU.subtract))
                chain(dve.tensor_scalar(small[:, 11 - c, 0:E], small[:, 11 - c, 0:E], float(P), None, ALU.mult))
                chain(dve.tensor_tensor(v3(2), v3(a), cnt, ALU.subtract))
                chain(dve.tensor_tensor(v3(2), v3(2), rank, ALU.add))
                chain(dve.tensor_tensor(v3(2), v3(2), small[:, 11 - c, 0:E].unsqueeze(1).broadcast_to([P, KT, E]), ALU.add))
                chain(dve.tensor_tensor(v3(2), v3(2), ohb[:, 0:KT, :], ALU.mult))
                chain(dve.tensor_reduce(small[:, 7, 0:KT], v3(2), AX.X, ALU.add))
                dve.tensor_copy(pos[:, 0:KT], small[:, 7, 0:KT]).then_inc(s["pos_ready"], 1)

                def row_max(b, g, n):
                    h, qt = n // TB, n % TB
                    (wait_apart(dve, s["s_ready"], 16 * (4 * b + g) + n + 1, passed_dve) if L == 0 else
                     dve.wait_ge(s["s_ready"], 16 * (4 * b + g) + n + 1))
                    if L == 0:
                        N = (qt + 1) * P
                        dve.tensor_tensor_reduce(dump[:, n % 2, 0:N], ps[:, 4 + n % 2, 0:N], cst[:, C_MASK + 512 - N:C_MASK + 512],
                                                 1.0, -3.0e38, ALU.add, ALU.max, mx[:, g, h, qt:qt + 1]
                                                 ).then_inc(s["s_used"], 1)
                    else:
                        dve.tensor_reduce(mx[:, g, h, qt:qt + 1], ps[:, 4 + n % 2, :], AX.X, ALU.max
                                          ).then_inc(s["s_used"], 1)

                def m_lo(b, g):
                    dve.wait_ge(s["mh_ready"], NB * NG * L + 4 * b + g + 1)
                    wait(dve, s[f"min{g}"], BASE[L] + 32 * b)
                    dve.tensor_tensor(mlo[:, g, :], ps[0:G * TB, 7, 0:P], mhi[:, g, :], ALU.subtract
                                      ).then_inc(s["ml_ready"], 1)

                def normalize(b, g):
                    t = 4 * b + g
                    dve.wait_ge(s["oT_done"], t + 1)
                    oT = ps[:, 7, :].rearrange("p (q h w) -> p q h w", q=TB, h=G)
                    dve.reciprocal(rec[:, :, :], oT[:, :, :, DH]).then_inc(s["rec_ready"], 1)
                    dve.wait_ge(s["rec_ready"], t + 1)
                    dst = o_sb[:, bass.ds(b * TB, TB), g * G * DH:(g + 1) * G * DH].rearrange("p q (h d) -> p q h d", h=G)
                    dve.tensor_tensor(dst, oT[:, :, :, 0:DH], rec[:, :, :].unsqueeze(3).broadcast_to([P, TB, G, DH]),
                                      ALU.mult).then_inc(s["norm_done"], 1)

                def prev(b, g):
                    return (b, g - 1) if g else (b - 1, NG - 1)

                def slot(b, g, more, last):
                    for kt in range(TB):
                        for hp in (0, 1):
                            if more:
                                for n in range(4 * kt + 2 * hp, 4 * kt + 2 * hp + 2):
                                    row_max(b + (g + 2) // NG, (g + 2) % NG, n)
                            if (kt, hp) == (1, 1) and not last:
                                m_lo(b + (g + 1) // NG, (g + 1) % NG)
                            if (kt, hp) == (3, 0) and not (isinstance(b, int) and b == 0 and g == 0):
                                normalize(*prev(b, g))
                for g in (0, 1):
                    for n in range(16):
                        row_max(0, g, n)
                m_lo(0, 0)
                for g in range(NG):
                    slot(0, g, True, False)
                with dve.Fori(1, NB - 1) as b:
                    for g in range(NG):
                        slot(b, g, True, False)
                for g in range(NG):
                    slot(NB - 1, g, g < 2, g == NG - 1)
                normalize(NB - 1, NG - 1)

                def head(par, jn):
                    dve.wait_ge(s["xeT_psum"], jn + 1)
                    wait(dve, s["h_psum"], jn)
                    if L == 0:
                        dve.wait_ge(s[f"we{par}"], 16 * ((jn // 2 if isinstance(jn, int) else jn2[0]) + 1))
                        dve.tensor_scalar(xeT[:, par, :], ps[:, 0, 0:P], we[:, par, W_G:W_G + 1],
                                          we[:, par, W_LB:W_LB + 1], ALU.mult, ALU.add).then_inc(s["xeT_ready"], 1)
                    else:
                        dve.tensor_copy(xeT[:, par, :], ps[:, 0, 0:P]).then_inc(s["xeT_ready"], 1)

                def bias1(par, jn):
                    dve.wait_ge(s["h_psum"], jn + 1)
                    wait(dve, s["h_ready"], jn)
                    dve.tensor_tensor(hb[:, :, :], ps[:, 1, :].rearrange("p (c t) -> p c t", c=FC),
                                      we[:, par, W_B1:W_B1 + FC].unsqueeze(2).broadcast_to([P, FC, P]), ALU.add
                                      ).then_inc(s["hb_ready"], 1)

                def bias2(par, jn, first):
                    dve.wait_ge(s["mm2_done"], jn + 1)
                    if not first:
                        wait(dve, s[f"yo{par}"], 16 * jn2[0])
                    dve.tensor_tensor(ye[:, par, :], ps[:, 2 + par, 0:P], we[:, par, W_B2:W_B2 + P], ALU.add
                                      ).then_inc(s["ye_ready"], 1)
                jn2 = [0]
                head(0, 0)
                bias1(0, 0)

                def step(jj):
                    jn2[0] = jj
                    head(1, 2 * jj + 1)
                    bias1(1, 2 * jj + 1)
                    bias2(0, 2 * jj, False)
                    jn2[0] = jj + 1
                    head(0, 2 * jj + 2)
                    bias1(0, 2 * jj + 2)
                    jn2[0] = jj
                    bias2(1, 2 * jj + 1, False)
                each(dve, SLOTS[L] // 2 - 1, step)
                n = SLOTS[L] - 2
                jn2[0] = n // 2
                head(1, n + 1)
                bias1(1, n + 1)
                bias2(0, n, False)
                bias2(1, n + 1, False)

                dve.wait_ge(s["gathered"], 16 * KT)

                def step(b):
                    bs = bass.ds(b * TB, TB)
                    z = hb[:, :, :]
                    if L == 0:
                        wait(dve, s["silu_ready"], b)
                        dve.tensor_tensor(z, yg_sb[:, bs, :], xn_sb[:, bs, :], ALU.add).then_inc(s["z_ready"], 1)
                        sv = ps[:, 6, :].rearrange("p (a c) -> p a c", a=TB)
                        dve.wait_ge(s["s_psum"], b + 1)
                    else:
                        wait(dve, s["silu_ready"], b)
                        wait(dve, s["x_ready"], b)
                        w = lambda k: wch[:, k, bs].unsqueeze(2).broadcast_to([P, TB, P])
                        dve.tensor_tensor(hT[:, 1], yg_sb[:, bs, :], w(0), ALU.mult).then_inc(s["chain_a"], 1)
                        dve.tensor_tensor(z, v_sb[:, bs, :], w(1), ALU.mult).then_inc(s["chain_a"], 1)
                        dve.wait_ge(s["chain_a"], NB * TB + 3 * b + 2)
                        dve.tensor_tensor(hT[:, 1], hT[:, 1], z, ALU.add).then_inc(s["chain_a"], 1)
                        dve.wait_ge(s["chain_a"], NB * TB + 3 * b + 3)
                        dve.tensor_tensor(z, hT[:, 1], xn_sb[:, bs, :], ALU.add).then_inc(s["z_ready"], 1)
                        sv = o_sb[:, bs, :]
                    dve.wait_ge(s["silu_ready"], b + 1)
                    dve.tensor_tensor(hT[:, 1], hT[:, 0], sv, ALU.mult).then_inc(s["sg_ready"], 1)
                    dve.wait_ge(s["sg_ready"], b + 1)
                    dve.tensor_tensor(x_sb[:, bs, :], x_sb[:, bs, :], hT[:, 1], ALU.add).then_inc(s["x_ready"], 1)
                each(dve, NB, step)
                dve.wait_ge(s["x_ready"], NB)


_INS = ["x", "rope", "const", "w0", "w1", "e0", "e1"]
_OUTS = [((8, 512, 128), 'float32')]


def layout(np, i):
    a = {k: np.asarray(v) for k, v in i.items()}
    f32 = np.float32
    r = np.arange(P)
    order = (r % H) * DH + r // H
    swapped = (r % H) * DH + ((r // H) ^ 1)
    wq, wk = a["L0_attn_wq"], a["L0_attn_wk"]
    w0 = np.concatenate([wq[order].T, wq[swapped].T, wk[order].T, wk[swapped].T, a["L0_attn_wv"].T, a["L0_attn_wo"].T,
                         a["L0_ffn_centroids"].T], axis=1)
    chunks = lambda w: w.reshape(FC, P, P).transpose(1, 0, 2).reshape(P, F)
    everywhere = lambda v: np.broadcast_to(v[None, :], (P, P))
    w1 = np.concatenate([a["L1_attn_Wq"][:, order], a["L1_attn_Wk"][:, order], a["L1_attn_Wk"], a["L1_ffn_gate_w"].T,
                         a["L1_ffn_sw_in"], chunks(a["L1_ffn_sw_out"]), a["L1_attn_bq"][order][:, None],
                         a["L1_attn_bk"][order][:, None], everywhere(a["L1_attn_bk"]),
                         a["L1_ffn_sb_in"].reshape(FC, P).T, everywhere(a["L1_ffn_sb_out"])], axis=1)

    def experts(W1, W2, b1, b2, *more):
        return np.ascontiguousarray(np.stack([np.concatenate(
            [W1[e], chunks(W2[e]), b1[e].reshape(FC, P).T, everywhere(b2[e])] + [m[e][:, None] for m in more], axis=1)
            for e in range(E)]))
    e0 = experts(a["L0_ffn_W1"], a["L0_ffn_W2"], a["L0_ffn_b1"], a["L0_ffn_b2"], a["L0_ffn_ln_g"], a["L0_ffn_ln_b"])
    e1 = experts(a["L1_ffn_w_in"], a["L1_ffn_w_out"], a["L1_ffn_b_in"], a["L1_ffn_b_out"])
    d = r // H
    freq = (f32(1.0) / f32(10000.0) ** (np.arange(0, DH, 2, dtype=f32) / f32(DH))).astype(f32)
    ang = np.outer(freq[d // 2], np.arange(TB * P, dtype=f32)).astype(f32)
    rope = np.stack([np.cos(ang), np.where(d % 2 == 0, -1, 1)[:, None] * np.sin(ang)], axis=1).astype(f32)
    const = np.zeros((P, NCONST), f32)
    const[:, C_ID:C_ID + P] = np.eye(P)
    const[:, C_UP:C_UP + P] = r[:, None] < r[None, :]
    const[:, C_ONE:C_ONE + P] = 1
    const[:, C_MASK + 384:C_MASK + 512] = np.where(r[None, :] > r[:, None], -BIG, 0)
    const[:, C_DESC:C_DESC + E] = E - np.arange(E)
    const[:, C_J128:C_J128 + NT] = P * np.arange(NT)
    const[:, C_J:C_J + SLOTS[1]] = np.arange(SLOTS[1])
    const[:, C_NHALF:C_NHALF + TB] = -0.5
    return [a["L0_attn_x"], rope, const, w0, w1, e0, e1]


def kernel(**inputs):
    import numpy as _np
    import concourse.bacc as _bacc
    from concourse import mybir as _mybir
    from concourse.bass_utils import run_bass_kernel_spmd as _run

    nc = _bacc.Bacc("TRN2", target_bir_lowering=False, num_devices=1)
    arrays, args = {}, []
    for name, a in zip(_INS, layout(_np, inputs)):
        a = _np.ascontiguousarray(a)
        arrays[f"in_{name}_dram"] = a
        args.append(nc.dram_tensor(f"in_{name}_dram", a.shape, _mybir.dt.from_np(a.dtype), kind="ExternalInput").ap())
    for i, (shape, dtype) in enumerate(_OUTS):
        dt = _mybir.dt.from_np(_np.dtype(dtype))
        args.append(nc.dram_tensor(f"out_{i}_dram", shape, dt, kind="ExternalOutput").ap())
    build(nc, *args)
    r = _run(nc, [arrays], core_ids=[0])
    got = tuple(r.results[0][f"out_{i}_dram"] for i in range(len(_OUTS)))
    return got[0]
```

```python
from contextlib import ExitStack

import concourse.bass as bass
from concourse import mybir

F32 = mybir.dt.float32
BF16 = mybir.dt.bfloat16
U32 = mybir.dt.uint32
I32 = mybir.dt.int32
ALU = mybir.AluOpType
ACT = mybir.ActivationFunctionType
AX = mybir.AxisListType

P = 128
NB = 8
TB = 4
NT = NB * TB
H = 16
DH = 8
E = 8
F = 512
FC = F // P
G = 4
NG = H // G
VW = 32
KS = 48
KM = 50
EPS = 1e-5
BIG = 1e30
CHOICES = (1, 2)
U = 256
UT = U // P
UNITS = (24, 40)
SCALE = (DH ** -0.5, P ** -0.5)
PARTS = ((0, 0, 1, 0, 2, 1), (0, 1, 0, 2, 0, 1))

C_ID, C_UP, C_ONE, C_MASK = 0, 128, 256, 384
C_DESC, C_JU, C_J, C_NHALF = 896, 904, 920, 960
NCONST = 964
UE = NT * P // U
W_2, W_B2, W_1 = 0, F, F + P
W_B1, W_G, W_LB = W_1 + F, W_1 + F + FC, W_1 + F + FC + 1
NW = (W_LB + 1, W_G)


def wait(eng, sem, value):
    if isinstance(value, int) and value <= 0:
        return
    eng.wait_ge(sem, value)


def each(eng, n, body):
    body(0)
    with eng.Fori(1, n) as i:
        body(i)


def wait_apart(eng, sem, value, passed):
    eng.wait_ge(sem, value)
    if not isinstance(value, int):
        eng.sem_inc(passed, 1)


def build(nc, x_in, rope_in, const_in, w0_in, w1_in, e0_in, e1_in, out):
    ctx = ExitStack()
    with ctx:
        def sb(name, shape, dt=F32):
            return ctx.enter_context(nc.sbuf_tensor(name, shape, dt))

        def pb(name, shape, dt=F32):
            return ctx.enter_context(nc.psum_tensor(name, shape, dt))

        def sem(name):
            return ctx.enter_context(nc.semaphore(name))

        def dram(name, shape, dt):
            return nc.dram_tensor(name, shape, dt, kind="Internal").ap()

        epack = (e0_in, e1_in)
        qk_d = [dram(f"qk_d{L}", [2, NB, 6 * DH, H, TB * P], BF16) for L in (0, 1)]
        xs_d = [dram(f"xs_d{L}", [UNITS[L] * U, P], F32) for L in (0, 1)]
        ys_d = [dram(f"ys_d{L}", [UNITS[L] * U, P], F32) for L in (0, 1)]

        zq_d = dram("zq_d", [2, G, TB * P], BF16)

        cst = sb("cst", [P, NCONST])
        rope = sb("rope", [P, 2, TB * P])
        w0 = sb("w0", [P, 6 * P + E])
        w1 = sb("w1", [P, 3 * P + E + 2 * F + 2 + P + FC + P])
        idb = cst[:, C_ID:C_ID + P]
        upb = sb("upb", [P, P], BF16)
        oneb = sb("oneb", [P, P], BF16)
        x_sb = sb("x_sb", [P, NT, P])
        xn_sb = sb("xn_sb", [P, NT, P])
        xs_sb = sb("xs_sb", [P, NT, P])
        v_sb = sb("v_sb", [P, NT, P])
        o_sb = sb("o_sb", [P, NT, P])
        yg_sb = sb("yg_sb", [P, NT, P])
        ptmp = yg_sb[:, :, :].rearrange("p a b -> p (a b)").rearrange("p (k s t) -> p k s t", k=4, s=2)
        cosq, sinq, qf, r1 = (ptmp[:, k] for k in range(4))
        parts = [sb(f"part{k}", [P, 2, TB * P], BF16) for k in range(3)]
        mv = sb("mv", [P, 2, TB, 2])
        st6 = sb("st6", [P, TB, 6])
        rstd = sb("rstd", [P, 2, TB])
        vare = sb("vare", [P, 2, TB])
        xns = sb("xns", [P, TB, P])
        xT = sb("xT", [P, TB * P])
        lg = sb("lg", [P, NT, E])
        Qs = sb("Qs", [P, NG, G, TB * P], BF16)
        Ks = sb("Ks", [P, NG, G, TB * P], BF16)
        PT = sb("PT", [P, 2, G, TB * P])
        hsh = PT[:, :, :, :]
        Vs = sb("Vs", [P, NG, TB, G, VW])
        mx = sb("mx", [P, NG, G, TB])
        mhi = sb("mhi", [G * TB, NG, P], BF16)
        mlo = sb("mlo", [G * TB, NG, P], BF16)
        dump = sb("dump", [P, 2, TB * P], BF16)
        oc = xT
        rec = sb("rec", [P, TB, G])
        big = PT[:, :, :, :].rearrange("p k h t -> p (k h) t")
        small = sb("small", [P, 8, 2 * NT])
        ohb = sb("ohb", [P, 2 * NT, E], BF16)
        pos = sb("pos", [P, 2 * NT], U32)
        tex = sb("tex", [P, UNITS[1]], I32)
        wch = sb("wch", [P, 2, NT])
        zero = sb("zero", [P, P])
        we = sb("we", [P, 2, NW[0]])
        xe = sb("xe", [P, 2, UT, P])
        xeT = sb("xeT", [P, 2, U])
        flat = PT[:, :, :, :].rearrange("p k h t -> p (k h t)").rearrange("p (k r c u) -> p k r c u", k=2, r=2, c=FC)
        hb, hT = flat[:, 0], flat[:, 1]
        ye = sb("ye", [P, 2, UT, P])
        zb = PT[:, 0, 0, :].rearrange("p (a c) -> p a c", a=TB)
        zs = PT[:, 0, 1, :].rearrange("p (a c) -> p a c", a=TB)
        zg = PT[:, 0, 2, :].rearrange("p (a c) -> p a c", a=TB)
        xn2s = zb

        ps = pb("ps", [P, 8, 512])

        s_load = sem("inputs_loaded")
        s_const = sem("constants_ready")
        s_setup = sem("setup_done")
        S = []
        LOADS = {n: sem(n) for n in "ld0 ld1 ld2 ld3 min0 min1 min2 min3 mT_ready mh_ready ml_ready".split()}
        BASE = (0, 32 * NB)
        for L in (0, 1):
            names = """chain_v chain_g chain_a x_stats rstd_ready xn_ready xn2_stats rstd2_ready xn2_ready xn_saved xT_psum xT_ready
                mm_q0 mm_q1 mm_v mm_lg rope_q0 rope_q1 qf_0 qf_1 p1_0 p1_1 r1_0 r1_1 p2_0 p2_1 p3_0 p3_1 out_0 out_1
                v_saved lg_saved rec_ready sh_psum sh_h sh_y sh_saved
                onehot_ready counts_ready pos_ready gate_exp zeroed scattered tiles_ready
                ld0 ld1 ld2 ld3 min0 min1 min2 min3 s_ready s_used mT_ready mh_ready ml_ready st_ready exp_done masked pv_done
                o_copied oT_done norm_done v_ready
                wu0 wu1 wd0 wd1 xe0 xe1 xeT_psum xeT_ready h_psum hb_ready h_ready mm2_done ye_ready yo0 yo1 gathered
                og oT2_psum oT2_ready s_psum z_ready silu_ready sg_ready x_ready""".split()
            unused = ("sh_psum sh_h sh_y sh_saved gate_exp", "xn2_stats rstd2_ready xn2_ready rope_q0 rope_q1 masked og oT2_psum oT2_ready s_psum")
            S.append({n: sem(f"{n}_{L}") for n in names if n not in unused[L].split() and n not in LOADS})
            S[L].update(LOADS)
        s_out = sem("out_stored")
        passed_dve = sem("passed_dve")
        passed_pool = passed_gpsimd = passed_dve
        block = ctx.enter_context(nc.Block())

        rows = lambda ap: ap.rearrange("(n p) d -> p n d", p=P)

        def mask_blocks(L, kt):
            return kt * P if L == 0 else 0

        @block.sync
        def _(sp):
            xr = x_in.rearrange("b (n p) d -> p (b n) d", p=P)
            for b in range(0, NT, 8):
                sp.dma_start(x_sb[:, b:b + 8, :], xr[:, b:b + 8, :]).then_inc(s_load, 16)
            sp.dma_start(cst[:, :], const_in).then_inc(s_load, 16)
            sp.dma_start(w0[:, :], w0_in).then_inc(s_load, 16)
            sp.dma_start(w1[:, :], w1_in).then_inc(s_load, 16)
            sp.dma_start(rope[:, :, :], rope_in).then_inc(s_load, 16)
            sp.wait_ge(s_setup, 2)
            sp.dma_start(zq_d, Qs[KS:KM, 0, :, :]).then_inc(s_load, 16)
            sp.wait_ge(s_load, 16 * 9)
            for L in (0, 1):
                s = S[L]
                for j in range(0, UNITS[L] * UT, 8):
                    sp.dma_start(rows(xs_d[L])[:, j:j + 8, :], zero[:, :].unsqueeze(1).broadcast_to([P, 8, P])).then_inc(s["zeroed"], 16)

                def step(b):
                    at = bass.ds(sp.snap(b * TB), TB)
                    sp.wait_ge(s["xn_ready"], TB * b + TB)
                    if L == 0:
                        sp.wait_ge(s["xn2_ready"], TB * b + TB)
                        sp.dma_start(xn_sb[:, at, :], xns[:, :, :]).then_inc(s["xn_saved"], 16)
                        sp.dma_start(xs_sb[:, at, :], xn2s[:, :, :]).then_inc(s["xn_saved"], 16)
                    else:
                        sp.dma_start(xs_sb[:, at, :], xns[:, :, :]).then_inc(s["xn_saved"], 16)
                    for i in (0, 1):
                        dst = qk_d[L][i, bass.ds(b, 1)].rearrange("o (c d) h t -> c (o d h) t", c=6)
                        for k in range(3):
                            sp.wait_ge(s[f"p{k + 1}_{i}"], b + 1)
                            for c in range(6):
                                if PARTS[i][c] == k:
                                    sp.dma_start(dst[c], parts[k][:, i, :]).then_inc(s[f"out_{i}"], 16)
                each(sp, NB, step)
                for i in (0, 1):
                    sp.wait_ge(s[f"out_{i}"], 16 * 6 * NB)

                def load(b, g):
                    wait(sp, s["exp_done"], 8 * (4 * b + g - 4) + 8)
                    bb = bass.ds(b, 1)
                    for dstk, i in ((Qs, 0), (Ks, 1)):
                        src = qk_d[L][i, bb, :, g * G:(g + 1) * G, :].rearrange("o r h t -> (o r) h t")
                        sp.dma_start(dstk[0:KS, g, :, :], src).then_inc(s[f"ld{g}"], 16)
                    sp.dma_start(Qs[KS:KM, g, :, :], zq_d).then_inc(s[f"ld{g}"], 16)

                def maxima(b, g):
                    sp.wait_ge(s["ml_ready"], NB * NG * L + 4 * b + g + 1)
                    for r, m in ((KS, mhi), (KS + 1, mlo)):
                        dst = Qs[r:r + 1, g, :, :].rearrange("o h (q t) -> o (h q) t", t=P)
                        sp.dma_start(dst, m[:, g, :]).then_inc(s[f"min{g}"], 16)

                for g in range(NG):
                    load(0, g)
                maxima(0, 0)

                def slot(b, g, more, last):
                    if not last:
                        maxima(b + (g + 1) // NG, (g + 1) % NG)
                    if more:
                        load(b + 1, g)
                for g in range(NG):
                    slot(0, g, True, False)
                with sp.Fori(1, NB - 1) as b:
                    for g in range(NG):
                        slot(b, g, True, False)
                for g in range(NG):
                    slot(NB - 1, g, False, g == NG - 1)
                sp.wait_ge(s["tiles_ready"], 1)
                sp.wait_ge(s["scattered"], 16 * CHOICES[L] * NT)
                units = lambda ap: ap.rearrange("(j n p) d -> j p n d", p=P, n=UT)

                def expert(j, lo, hi):
                    e = sp.value_load(tex[0:1, bass.ds(j, 1)], min_val=0, max_val=E - 1)
                    return epack[L][bass.ds(e, 1), :, lo:hi].rearrange("o p n -> (o p) n")

                def feed_up(j, par):
                    src = expert(j, W_1, NW[L])
                    wait(sp, s["hb_ready"], j - 1)
                    sp.dma_start(we[:, par, W_1:NW[L]], src).then_inc(s[f"wu{par}"], 16)
                    sp.dma_start(xe[:, par, :, :], units(xs_d[L])[bass.ds(j, 1)].rearrange("o p n d -> (o p) n d")
                                 ).then_inc(s[f"xe{par}"], 16)

                def feed_down(j, par):
                    src = expert(j, 0, W_1)
                    wait(sp, s["ye_ready"], j - 1)
                    sp.dma_start(we[:, par, 0:W_1], src).then_inc(s[f"wd{par}"], 16)

                def drain(j, par):
                    sp.wait_ge(s["ye_ready"], j + 1)
                    sp.dma_start(units(ys_d[L])[bass.ds(j, 1)].rearrange("o p n d -> (o p) n d"), ye[:, par, :, :]
                                 ).then_inc(s[f"yo{par}"], 16)

                for j in (0, 1):
                    feed_up(j, j)
                    feed_down(j, j)
                feed_up(2, 0)
                feed_up(3, 1)

                def step(jj):
                    for par in (0, 1):
                        feed_down(jj * 2 + par + 2, par)
                        drain(jj * 2 + par, par)
                        feed_up(jj * 2 + par + 4, par)
                each(sp, UNITS[L] // 2 - 2, step)
                for par in (0, 1):
                    feed_down(UNITS[L] - 2 + par, par)
                    drain(UNITS[L] - 4 + par, par)
                for par in (0, 1):
                    drain(UNITS[L] - 2 + par, par)
                if L == 0:

                    def step(b):
                        sp.wait_ge(s["norm_done"], NB * NG)
                        wait(sp, s["oT2_psum"], b)
                        sp.dma_start(xns[:, :, :], o_sb[:, bass.ds(b * TB, TB), :]).then_inc(s["og"], 16)
                    each(sp, NB, step)
                else:
                    outr = out.rearrange("b (n p) d -> p (b n) d", p=P)
                    for b in range(NB):
                        sp.wait_ge(s["x_ready"], b + 1)
                        sp.dma_start(outr[:, b * TB:(b + 1) * TB, :], x_sb[:, b * TB:(b + 1) * TB, :]).then_inc(s_out, 16)
                    sp.wait_ge(s_out, 16 * NB)

        @block.gpsimd
        def _(pool):
            pool.memset(zero[:, :], 0.0).then_inc(s_setup, 1)
            pool.wait_ge(s_load, 16 * 8)
            for L in (0, 1):
                s = S[L]

                def rsqrt(b, k, stats, ready):
                    wait_apart(pool, s[stats], b + 1, passed_pool)
                    pool.tensor_scalar(vare[:, k, :], mv[:, k, :, 1], EPS, None, ALU.add).then_inc(s["chain_g"], 1)
                    pool.wait_ge(s["chain_g"], (b * (2 if L == 0 else 1) + k) + 1)
                    pool.tensor_tensor(rstd[:, k, :], vare[:, k, :], cst[:, C_NHALF:C_NHALF + TB], ALU.pow
                                       ).then_inc(s[ready], 1)

                def norm(b):
                    rsqrt(b, 0, "x_stats", "rstd_ready")
                    if L == 0:
                        rsqrt(b, 1, "xn2_stats", "rstd2_ready")

                def split(b):
                    for i in (0, 1):
                        if L == 0:
                            pool.wait_ge(s[f"rope_q{i}"], b + 1)
                            wait(pool, s[f"p3_{i}"], b)
                            wait(pool, s[f"r1_{i}"], b)
                            pool.tensor_tensor(qf[:, i, :], cosq[:, i, :], sinq[:, i, :], ALU.add
                                               ).then_inc(s[f"qf_{i}"], 1)
                    for i in (0, 1):
                        pool.wait_ge(s[f"p2_{i}"], b + 1)
                        wait(pool, s[f"out_{i}"], 16 * 6 * b)
                        pool.tensor_tensor(parts[2][:, i, :], r1[:, i, :], parts[1][:, i, :], ALU.subtract
                                           ).then_inc(s[f"p3_{i}"], 1)
                norm(0)

                def step(b):
                    norm(b + 1)
                    split(b)
                each(pool, NB - 1, step)
                split(NB - 1)
                pool.wait_ge(s["pos_ready"], 1)
                pool.wait_ge(s["zeroed"], 16 * UNITS[L] * UT // 8)
                pool.wait_ge(s["xn_saved"], 16 * NB * (2 if L == 0 else 1))

                def scatter(n):
                    pool.indirect_dma_start(xs_d[L], bass.IndirectOffsetOnAxis(ap=pos[:, n:n + 1], axis=0),
                                            xs_sb[:, n % NT, :], None).then_inc(s["scattered"], 16)

                def v_slot(b, g):
                    if not isinstance(b, int) or b:
                        wait_apart(pool, s["pv_done"], 4 * (4 * b + g - 4) + 4, passed_pool)
                    src = v_sb[:, bass.ds(b * TB, TB), g * G * DH:(g + 1) * G * DH].rearrange(
                        "p k (h d) -> p k h d", h=G)
                    pool.tensor_copy(Vs[:, g, :, :, 0:DH], src).then_inc(s["v_ready"], 1)

                def slot(b, g, more):
                    if more:
                        v_slot(b + (g + 2) // NG, (g + 2) % NG)
                    if L == 0:
                        for kt in range(TB):
                            for hp in (0, 1):
                                wait_apart(pool, s["exp_done"], 8 * (4 * b + g) + 2 * kt + hp + 1, passed_pool)
                                d = PT[:, kt % 2, 2 * hp:2 * hp + 2, kt * P:(kt + 1) * P]
                                pool.affine_select(out=d, in_=d, compare_op=ALU.is_ge, fill=0.0, base=0,
                                                   pattern=[[0, 2], [1, P]], channel_multiplier=-1
                                                   ).then_inc(s["masked"], 1)
                pool.wait_ge(s["v_saved"], NB)
                pool.wait_ge(s_setup, 2)
                v_slot(0, 0)
                v_slot(0, 1)
                for g in range(NG):
                    if L == 1:
                        for n in range(16 * g, 16 * g + 16):
                            scatter(n)
                    else:
                        for n in range(8 * g, 8 * g + 8):
                            scatter(n)
                    slot(0, g, True)
                with pool.Fori(1, NB - 1) as b:
                    for g in range(NG):
                        slot(b, g, True)
                for g in range(NG):
                    slot(NB - 1, g, g < 2)
                for par in (0, 1):
                    pool.wait_ge(s[f"yo{par}"], 16 * UNITS[L] // 2)
                pool.wait_ge(s["pv_done"], 4 * NB * NG)
                for n in range(CHOICES[L] * NT):
                    dst = (yg_sb if n < NT else v_sb)[:, n % NT, :]
                    pool.indirect_dma_start(dst, None, ys_d[L],
                                            bass.IndirectOffsetOnAxis(ap=pos[:, n:n + 1], axis=0)
                                            ).then_inc(s["gathered"], 16)

        @block.scalar
        def _(act):
            act.wait_ge(s_load, 16 * 8)
            for L in (0, 1):
                s = S[L]

                def x_T(b):
                    act.wait_ge(s["xT_psum"], b + 1)
                    wait(act, s["mm_lg"] if L == 0 else s["sh_psum"], b if L == 0 else FC * b)
                    act.copy(xT[:, :], ps[:, 7, :]).then_inc(s["xT_ready"], 1)

                def post(b):
                    for i in (0, 1):
                        if L == 1:
                            act.wait_ge(s[f"mm_q{i}"], b + 1)
                            wait(act, s[f"p3_{i}"], b)
                            wait(act, s[f"r1_{i}"], b)
                            act.activation(qf[:, i, :], ps[:, 2 * i, :], ACT.Identity,
                                           bias=w1[:, 3 * P + E + 2 * F + i:3 * P + E + 2 * F + i + 1]
                                           ).then_inc(s[f"qf_{i}"], 1)
                    for i in (0, 1):
                        act.wait_ge(s[f"qf_{i}"], b + 1)
                        wait(act, s[f"out_{i}"], 16 * 6 * b)
                        act.copy(parts[0][:, i, :], qf[:, i, :]).then_inc(s[f"p1_{i}"], 1)
                    if L == 0:
                        act.wait_ge(s["mm_v"], b + 1)
                        act.copy(v_sb[:, bass.ds(b * TB, TB), :],
                                 ps[:, 4, :].rearrange("p (a c) -> p a c", a=TB)).then_inc(s["v_saved"], 1)
                    for i in (0, 1):
                        act.wait_ge(s[f"r1_{i}"], b + 1)
                        act.copy(parts[1][:, i, :], r1[:, i, :]).then_inc(s[f"p2_{i}"], 1)
                    if L == 1:
                        for c in range(FC):
                            act.wait_ge(s["sh_psum"], FC * b + c + 1)
                            wait(act, s["sh_y"], b)
                            act.activation(hsh[:, 0, c, :], ps[:, 1 if c % 2 == 0 else 3, :], ACT.Gelu,
                                           bias=w1[:, C_SBIN + c:C_SBIN + c + 1]).then_inc(s["sh_h"], 1)
                if L == 1:
                    C_SBIN = 3 * P + E + 2 * F + 2 + P
                x_T(0)

                def step(b):
                    post(b)
                    x_T(b + 1)
                each(act, NB - 1, step)
                post(NB - 1)
                if L == 1:
                    act.wait_ge(s["gate_exp"], 1)
                    act.activation(big[:, 1, 0:NT * E], big[:, 0, 0:NT * E], ACT.Exp).then_inc(s["gate_exp"], 1)
                    act.wait_ge(s["gate_exp"], 3)
                    act.activation(small[:, 2, 0:NT], small[:, 2, 0:NT], ACT.Exp).then_inc(s["gate_exp"], 1)

                def m_hi(b, g):
                    act.wait_ge(s["mT_ready"], NB * NG * L + 4 * b + g + 1)
                    wait(act, s[f"min{g}"], BASE[L] + 32 * b)
                    act.copy(mhi[:, g, :], ps[0:G * TB, 7, 0:P]).then_inc(s["mh_ready"], 1)

                def o_copy(b, g):
                    act.wait_ge(s["pv_done"], 4 * (4 * b + g) + 4)
                    wait(act, s["oT_done"], 4 * b + g)
                    act.copy(oc[:, :], ps[:, 6, :]).then_inc(s["o_copied"], 1)

                def prev(b, g):
                    return (b, g - 1) if g else (b - 1, NG - 1)

                def slot(b, g, last):
                    for kt in range(TB):
                        for hp in (0, 1):
                            u = 8 * (4 * b + g) + 2 * kt + hp
                            act.wait_ge(s["st_ready"], u + 1)
                            wait(act, s["pv_done"], 4 * (4 * b + g) + kt - 1)
                            q0 = mask_blocks(L, kt)
                            k = 2 * (u % 2 if isinstance(u, int) else hp)
                            act.activation(PT[:, kt % 2, 2 * hp:2 * hp + 2, q0:], ps[:, 2 * hp:2 * hp + 2, q0:],
                                           ACT.Exp, scale=SCALE[L]).then_inc(s["exp_done"], 1)
                            if (kt, hp) == (0, 1) and not (isinstance(b, int) and b == 0 and g == 0):
                                o_copy(*prev(b, g))
                            if (kt, hp) == (1, 0) and not last:
                                m_hi(b + (g + 1) // NG, (g + 1) % NG)
                m_hi(0, 0)
                for g in range(NG):
                    slot(0, g, False)
                with act.Fori(1, NB - 1) as b:
                    for g in range(NG):
                        slot(b, g, False)
                for g in range(NG):
                    slot(NB - 1, g, g == NG - 1)
                o_copy(NB - 1, NG - 1)

                def step(jj):
                    for par in (0, 1):
                        j = jj * 2 + par
                        act.wait_ge(s["hb_ready"], j + 1)
                        wait(act, s["mm2_done"], j - 1)
                        act.activation(hT[:, par].rearrange("p c t -> p (c t)"), hb[:, par].rearrange("p c t -> p (c t)"),
                                       ACT.Relu if L == 0 else ACT.Gelu).then_inc(s["h_ready"], 1)
                each(act, UNITS[L] // 2, step)

                def step(b):
                    if L == 0:
                        act.wait_ge(s["oT2_psum"], b + 1)
                        wait(act, s["s_psum"], b)
                        act.copy(xT[:, :], ps[:, 7, :]).then_inc(s["oT2_ready"], 1)
                    act.wait_ge(s["z_ready"], b + 1)
                    wait(act, s["sg_ready"], b)
                    act.activation(zs, zb, ACT.Silu).then_inc(s["silu_ready"], 1)

                each(act, NB, step)
        @block.tensor
        def _(pe):
            pe.wait_ge(s_load, 16 * 8)
            pe.wait_ge(s_setup, 2)
            for L in (0, 1):
                s = S[L]
                if L == 1:
                    pe.wait_ge(S[0]["x_ready"], NB)

                def x_T(b):
                    pe.wait_ge(s["xn_ready"], TB * b + TB)
                    wait(pe, s["xT_ready"], b)
                    for n in range(TB):
                        mm = pe.transpose(ps[:, 7, n * P:(n + 1) * P], xns[:, n, :], idb)
                    mm.then_inc(s["xT_psum"], 1)

                def proj(b):
                    pe.wait_ge(s["xT_ready"], b + 1)
                    w = w0 if L == 0 else w1
                    for i in (0, 1):
                        if L == 0:
                            wait(pe, s[f"rope_q{i}"], b)
                            pe.matmul(ps[:, 2 * i, :], w[:, 2 * i * P:(2 * i + 1) * P], xT[:, :], start=True, stop=True)
                            mm = pe.matmul(ps[:, 2 * i + 1, :], w[:, (2 * i + 1) * P:(2 * i + 2) * P], xT[:, :],
                                           start=True, stop=True)
                        else:
                            wait(pe, s[f"qf_{i}"], b)
                            mm = pe.matmul(ps[:, 2 * i, :], w[:, i * P:(i + 1) * P], xT[:, :], start=True, stop=True)
                        mm.then_inc(s[f"mm_q{i}"], 1)
                    wait(pe, s["v_saved"], b)
                    wv = w0[:, 4 * P:5 * P] if L == 0 else w1[:, 2 * P:3 * P]
                    for n in range(TB):
                        mm = pe.matmul(ps[:, 4, n * P:(n + 1) * P], xT[:, n * P:(n + 1) * P], wv, start=True, stop=True)
                    mm.then_inc(s["mm_v"], 1)
                    wait(pe, s["lg_saved"], b)
                    wr = w0[:, 6 * P:6 * P + E] if L == 0 else w1[:, 3 * P:3 * P + E]
                    for n in range(TB):
                        mm = pe.matmul(ps[:, 5, n * E:(n + 1) * E], xT[:, n * P:(n + 1) * P], wr, start=True, stop=True)
                    mm.then_inc(s["mm_lg"], 1)
                    if L == 1:
                        sw = 3 * P + E
                        for c in range(FC):
                            wait(pe, s["sh_h"], FC * b + (c - 1 if c >= 2 else 0))
                            mm = pe.matmul(ps[:, 1 if c % 2 == 0 else 3, :], w1[:, sw + c * P:sw + (c + 1) * P], xT[:, :],
                                           start=True, stop=True)
                            mm.then_inc(s["sh_psum"], 1)

                def shared(b):
                    pe.wait_ge(s["sh_h"], FC * b + FC)
                    wait(pe, s["sh_saved"], b)
                    sw = 3 * P + E + F
                    for n in range(TB):
                        for c in range(FC):
                            mm = pe.matmul(ps[:, 6, n * P:(n + 1) * P], hsh[:, 0, c, n * P:(n + 1) * P],
                                           w1[:, sw + c * P:sw + (c + 1) * P], start=(c == 0), stop=(c == FC - 1))
                    mm.then_inc(s["sh_y"], 1)
                x_T(0)

                def step(b):
                    proj(b)
                    x_T(b + 1)
                    if L == 1:
                        shared(b)
                each(pe, NB - 1, step)
                proj(NB - 1)
                if L == 1:
                    shared(NB - 1)
                KT = CHOICES[L] * NT
                pe.wait_ge(s["onehot_ready"], 1)
                pe.matmul(ps[:, 0, 0:KT * E], upb[:, :], ohb[:, 0:KT, :].rearrange("p n e -> p (n e)"),
                          start=True, stop=True)
                pe.matmul(ps[:, 1, 0:KT * E], oneb[:, :], ohb[:, 0:KT, :].rearrange("p n e -> p (n e)"),
                          start=True, stop=True).then_inc(s["counts_ready"], 1)

                def first_pass(b, g, n):
                    h, qt = n // TB, n % TB
                    if n == 0:
                        pe.wait_ge(s[f"ld{g}"], BASE[L] // 2 * 3 + 48 * b + 48)
                    N = (qt + 1) * P if L == 0 else TB * P
                    wait(pe, s["s_used"], 16 * (4 * b + g) + n - 1)
                    pe.matmul(ps[:, 4 + n % 2, 0:N], Qs[:, g, h, qt * P:(qt + 1) * P], Ks[:, g, h, 0:N],
                              start=True, stop=True).then_inc(s["s_ready"], 1)

                def m_T(b, g):
                    pe.wait_ge(s["s_used"], 16 * (4 * b + g) + 16)
                    wait(pe, s["norm_done"], 4 * b + g - 2)
                    pe.transpose(ps[0:G * TB, 7, 0:P], mx[:, g].rearrange("p h q -> p (h q)"), idb
                                 ).then_inc(s["mT_ready"], 1)

                def o_T(b, g, last):
                    pe.wait_ge(s["o_copied"], 4 * b + g + 1)
                    if last:
                        pe.wait_ge(s["norm_done"], 4 * b + g)
                    else:
                        pe.wait_ge(s["ml_ready"], NB * NG * L + 4 * b + g + 3)
                    for n in range(TB):
                        mm = pe.transpose(ps[:, 7, n * P:(n + 1) * P], oc[:, n * P:(n + 1) * P], idb)
                    mm.then_inc(s["oT_done"], 1)

                def weighted_v(b, g, kt):
                    t = 4 * b + g
                    if L == 0:
                        pe.wait_ge(s["masked"], 8 * t + 2 * kt + 2)
                    else:
                        pe.wait_ge(s["exp_done"], 8 * t + 2 * kt + 2)
                    if kt == 0:
                        pe.wait_ge(s["v_ready"], t + 1)
                        wait(pe, s["o_copied"], t)
                    q0 = mask_blocks(L, kt)
                    for h in range(G):
                        mm = pe.matmul(ps[h * VW:(h + 1) * VW, 6, q0:], Vs[:, g, kt, h, :], PT[:, kt % 2, h, q0:],
                                       start=(kt == 0), stop=(kt == TB - 1), skip_group_check=True)
                    mm.then_inc(s["pv_done"], 1)

                def prev(b, g):
                    return (b, g - 1) if g else (b - 1, NG - 1)

                def slot(b, g, more, last):
                    first = isinstance(b, int) and b == 0 and g == 0
                    for kt in range(TB):
                        for hp in (0, 1):
                            u = 8 * (4 * b + g) + 2 * kt + hp
                            if kt == 0 and hp == 0:
                                pe.wait_ge(s[f"min{g}"], BASE[L] + 32 * b + 32)
                            wait(pe, s["exp_done"], u - 1)
                            q0 = mask_blocks(L, kt)
                            for h in (2 * hp, 2 * hp + 1):
                                mm = pe.matmul(ps[:, h, q0:], Ks[:, g, h, kt * P:(kt + 1) * P], Qs[:, g, h, q0:],
                                               start=True, stop=True)
                            mm.then_inc(s["st_ready"], 1)
                            if more:
                                for n in range(4 * kt + 2 * hp, 4 * kt + 2 * hp + 2):
                                    first_pass(b + (g + 2) // NG, (g + 2) % NG, n)
                            if hp == 1:
                                if kt:
                                    weighted_v(b, g, kt - 1)
                                elif not first:
                                    weighted_v(*prev(b, g), TB - 1)
                            if (kt, hp) == (1, 0) and not last:
                                m_T(b + (g + 1) // NG, (g + 1) % NG)
                            if (kt, hp) == (2, 0) and not first:
                                o_T(*prev(b, g), last)
                for g in (0, 1):
                    for n in range(16):
                        first_pass(0, g, n)
                m_T(0, 0)
                for g in range(NG):
                    slot(0, g, True, False)
                with pe.Fori(1, NB - 1) as b:
                    for g in range(NG):
                        slot(b, g, True, False)
                for g in range(NG):
                    slot(NB - 1, g, g < 2, g == NG - 1)
                weighted_v(NB - 1, NG - 1, TB - 1)
                pe.wait_ge(s["o_copied"], NB * NG)
                pe.wait_ge(s["norm_done"], NB * NG - 1)
                for n in range(TB):
                    mm = pe.transpose(ps[:, 7, n * P:(n + 1) * P], oc[:, n * P:(n + 1) * P], idb)
                mm.then_inc(s["oT_done"], 1)

                def turn(j, par):
                    pe.wait_ge(s[f"xe{par}"], 16 * (j // 2 + 1) if isinstance(j, int) else 16 * (half[0] + 1))
                    wait(pe, s["xeT_ready"], j - 1)
                    for n in range(UT):
                        mm = pe.transpose(ps[:, par, n * P:(n + 1) * P], xe[:, par, n, :], idb)
                    mm.then_inc(s["xeT_psum"], 1)

                def up(j, par):
                    pe.wait_ge(s["xeT_ready"], j + 1)
                    pe.wait_ge(s[f"wu{par}"], 16 * (j // 2 + 1) if isinstance(j, int) else 16 * (half[0] + 1))
                    wait(pe, s["hb_ready"], j - 1)
                    for c in range(FC):
                        mm = pe.matmul(ps[:, 2 + 2 * par + c // 2, c % 2 * U:(c % 2 + 1) * U],
                                       we[:, par, W_1 + c * P:W_1 + (c + 1) * P], xeT[:, par, :], start=True, stop=True)
                    mm.then_inc(s["h_psum"], 1)

                def down(j, par):
                    pe.wait_ge(s["h_ready"], j + 1)
                    pe.wait_ge(s[f"wd{par}"], 16 * (j // 2 + 1) if isinstance(j, int) else 16 * (half[0] + 1))
                    wait(pe, s["ye_ready"], j - 1)
                    for n in range(UT):
                        for c in range(FC):
                            mm = pe.matmul(ps[:, 6 + par, n * P:(n + 1) * P], hT[:, par, c, n * P:(n + 1) * P],
                                           we[:, par, W_2 + c * P:W_2 + (c + 1) * P], start=(c == 0), stop=(c == FC - 1))
                    mm.then_inc(s["mm2_done"], 1)
                half = [0]
                pe.wait_ge(s["norm_done"], NB * NG)
                turn(0, 0)
                turn(1, 1)
                up(0, 0)

                def step(jj):
                    half[0] = jj + 1
                    turn(jj * 2 + 2, 0)
                    half[0] = jj
                    up(jj * 2 + 1, 1)
                    down(jj * 2, 0)
                    half[0] = jj + 1
                    turn(jj * 2 + 3, 1)
                    up(jj * 2 + 2, 0)
                    half[0] = jj
                    down(jj * 2 + 1, 1)
                each(pe, UNITS[L] // 2 - 1, step)
                n = UNITS[L] - 2
                up(n + 1, 1)
                down(n, 0)
                down(n + 1, 1)
                if L == 0:

                    def step(b):
                        pe.wait_ge(s["og"], 16 * b + 16)
                        wait(pe, s["oT2_ready"], b)
                        for n in range(TB):
                            mm = pe.transpose(ps[:, 7, n * P:(n + 1) * P], xns[:, n, :], idb)
                        mm.then_inc(s["oT2_psum"], 1)
                        pe.wait_ge(s["oT2_ready"], b + 1)
                        wait(pe, s["sg_ready"], b)
                        for n in range(TB):
                            mm = pe.matmul(ps[:, 6, n * P:(n + 1) * P], xT[:, n * P:(n + 1) * P], w0[:, 5 * P:6 * P],
                                           start=True, stop=True)
                        mm.then_inc(s["s_psum"], 1)

                    each(pe, NB, step)
        @block.vector
        def _(dve):
            dve.wait_ge(s_load, 16 * 8)
            dve.tensor_copy(upb[:, :], cst[:, C_UP:C_UP + P]).then_inc(s_const, 1)
            dve.tensor_copy(oneb[:, :], cst[:, C_ONE:C_ONE + P]).then_inc(s_const, 1)
            dve.memset(Qs[:, :, :, :], 0.0).then_inc(s_const, 1)
            dve.memset(Ks[0:64, :, :, :], -1.0).then_inc(s_const, 1)
            dve.memset(Ks[64:P, :, :, :], 0.0).then_inc(s_const, 1)
            dve.memset(Vs[:, :, :, :, :], 0.0).then_inc(s_const, 1)
            dve.wait_ge(s_const, 6)
            dve.memset(Vs[:, :, :, :, DH:DH + 1].rearrange("p g k h o -> p (g k h) o"), 1.0).then_inc(s_setup, 1)
            for L in (0, 1):
                s = S[L]
                chained = [0]

                def chain(ins):
                    chained[0] += 1
                    ins.then_inc(s["chain_v"], 1)
                    dve.wait_ge(s["chain_v"], chained[0])

                def stats(b, k, src, ready, free, count):
                    for n in range(TB):
                        ins = dve.bn_stats(st6[:, n, :], src(n))
                        ins.then_inc(s[free], 1)
                    wait_apart(dve, s[free], count, passed_dve)
                    for n in range(TB):
                        ins = dve.bn_aggr(mv[:, k, n, :], st6[:, n, :])
                    ins.then_inc(s[ready], 1)

                def norm(b):
                    per = 2 * TB if L == 0 else TB
                    stats(b, 0, lambda n: x_sb[:, bass.ds(b * TB + n, 1), :].rearrange("p o d -> p (o d)"), "x_stats",
                          "chain_a", per * b + TB)
                    dve.wait_ge(s["rstd_ready"], b + 1)
                    wait(dve, s["xT_psum"], b)
                    wait(dve, s["xn_saved"], 16 * (2 if L == 0 else 1) * b)
                    for n in range(TB):
                        ins = dve.tensor_scalar(xns[:, n, :], x_sb[:, bass.ds(b * TB + n, 1), :].rearrange("p o d -> p (o d)"),
                                                mv[:, 0, n, 0:1], rstd[:, 0, n:n + 1], ALU.subtract, ALU.mult)
                        ins.then_inc(s["xn_ready"], 1)
                    if L == 0:
                        dve.wait_ge(s["xn_ready"], TB * b + TB)
                        stats(b, 1, lambda n: xns[:, n, :], "xn2_stats", "chain_a", per * b + 2 * TB)
                        dve.wait_ge(s["rstd2_ready"], b + 1)
                        for n in range(TB):
                            ins = dve.tensor_scalar(xn2s[:, n, :], xns[:, n, :], mv[:, 1, n, 0:1], rstd[:, 1, n:n + 1],
                                                    ALU.subtract, ALU.mult)
                            ins.then_inc(s["xn2_ready"], 1)

                def post(b):
                    for i in (0, 1):
                        if L == 0:
                            dve.wait_ge(s[f"mm_q{i}"], b + 1)
                            wait(dve, s[f"qf_{i}"], b)
                            dve.tensor_tensor(cosq[:, i, :], ps[:, 2 * i, :], rope[:, 0, :], ALU.mult)
                            dve.tensor_tensor(sinq[:, i, :], ps[:, 2 * i + 1, :], rope[:, 1, :], ALU.mult
                                              ).then_inc(s[f"rope_q{i}"], 1)
                    if L == 1:
                        dve.wait_ge(s["mm_v"], b + 1)
                        bk = w1[:, 3 * P + E + 2 * F + 2:3 * P + E + 2 * F + 2 + P].unsqueeze(1).broadcast_to([P, TB, P])
                        dve.tensor_tensor(v_sb[:, bass.ds(b * TB, TB), :], ps[:, 4, :].rearrange("p (a c) -> p a c", a=TB),
                                          bk, ALU.add).then_inc(s["v_saved"], 1)
                    dve.wait_ge(s["mm_lg"], b + 1)
                    dve.tensor_copy(lg[:, bass.ds(b * TB, TB), :], ps[:, 5, 0:TB * E].rearrange("p (a e) -> p a e", a=TB)
                                    ).then_inc(s["lg_saved"], 1)
                    for i in (0, 1):
                        dve.wait_ge(s[f"p1_{i}"], b + 1)
                        wait(dve, s[f"p3_{i}"], b)
                        wait(dve, s[f"p2_{i}"], b)
                        dve.tensor_tensor(r1[:, i, :], qf[:, i, :], parts[0][:, i, :], ALU.subtract
                                          ).then_inc(s[f"r1_{i}"], 1)
                    if L == 1:
                        dve.wait_ge(s["sh_y"], b + 1)
                        sbo = w1[:, 3 * P + E + 2 * F + 2 + P + FC:3 * P + E + 2 * F + 2 + P + FC + P].unsqueeze(1).broadcast_to([P, TB, P])
                        dve.tensor_tensor(xn_sb[:, bass.ds(b * TB, TB), :], ps[:, 6, :].rearrange("p (a c) -> p a c", a=TB),
                                          sbo, ALU.add).then_inc(s["sh_saved"], 1)
                norm(0)

                def step(b):
                    norm(b + 1)
                    post(b)
                each(dve, NB - 1, step)
                post(NB - 1)

                K = CHOICES[L]
                KT = K * NT
                dve.wait_ge(s["lg_saved"], NB)
                dve.wait_ge(s["xn_saved"], 16 * NB * (2 if L == 0 else 1))

                def v3(k, n=KT):
                    return big[:, k, 0:n * E].rearrange("p (n e) -> p n e", e=E)

                def bc(ap, n):
                    return ap.unsqueeze(2).broadcast_to([P, n, E])
                desc = cst[:, C_DESC:C_DESC + E].unsqueeze(1).broadcast_to([P, NT, E])
                src = lg[:, :, :]
                for k in range(K):
                    top = small[:, k, 0:NT]
                    chain(dve.tensor_reduce(top, src, AX.X, ALU.max))
                    chain(dve.tensor_tensor(v3(0, NT), src, bc(top, NT), ALU.is_equal))
                    chain(dve.tensor_tensor(v3(0, NT), v3(0, NT), desc, ALU.mult))
                    chain(dve.tensor_reduce(small[:, 2, 0:NT], v3(0, NT), AX.X, ALU.max))
                    chain(dve.tensor_tensor(ohb[:, k * NT:(k + 1) * NT, :], desc, bc(small[:, 2, 0:NT], NT), ALU.is_equal))
                    if k + 1 < K:
                        chain(dve.tensor_scalar(v3(1, NT), ohb[:, 0:NT, :], -BIG, None, ALU.mult))
                        chain(dve.tensor_tensor(v3(3, NT), lg[:, :, :], v3(1, NT), ALU.add))
                        src = v3(3, NT)
                dve.sem_inc(s["onehot_ready"], 1)
                if L == 1:
                    chain(dve.tensor_tensor(v3(0, NT), lg[:, :, :], bc(small[:, 0, 0:NT], NT), ALU.subtract))
                    dve.sem_inc(s["gate_exp"], 1)
                    dve.wait_ge(s["gate_exp"], 2)
                    chain(dve.tensor_reduce(small[:, 3, 0:NT], v3(1, NT), AX.X, ALU.add))
                    chain(dve.tensor_tensor(small[:, 2, 0:NT], small[:, 1, 0:NT], small[:, 0, 0:NT], ALU.subtract))
                    dve.sem_inc(s["gate_exp"], 1)
                    dve.wait_ge(s["gate_exp"], 4)
                    chain(dve.reciprocal(wch[:, 0, :], small[:, 3, 0:NT]))
                    chain(dve.tensor_tensor(wch[:, 1, :], small[:, 2, 0:NT], wch[:, 0, :], ALU.mult))
                dve.wait_ge(s["counts_ready"], 1)
                cnt = ps[:, 1, 0:KT * E].rearrange("p (n e) -> p n e", e=E)
                rank = ps[:, 0, 0:KT * E].rearrange("p (n e) -> p n e", e=E)
                chain(dve.tensor_copy(v3(0), cnt))
                a, d = 0, 1
                while d < KT:
                    chain(dve.tensor_copy(v3(1 - a)[:, 0:d, :], v3(a)[:, 0:d, :]))
                    chain(dve.tensor_tensor(v3(1 - a)[:, d:KT, :], v3(a)[:, d:KT, :], v3(a)[:, 0:KT - d, :], ALU.add))
                    a, d = 1 - a, 2 * d
                total = v3(a)[:, KT - 1, :]
                tile_of = big[:, 3, 0:E * UE].rearrange("p (e j) -> p e j", e=E)
                chain(dve.tensor_tensor(tile_of, total.unsqueeze(2).broadcast_to([P, E, UE]),
                                        cst[:, C_JU:C_JU + UE].unsqueeze(1).broadcast_to([P, E, UE]), ALU.is_gt))
                chain(dve.tensor_reduce(small[:, 4, 0:E], tile_of, AX.X, ALU.add))
                chain(dve.tensor_copy(small[:, 5, 0:E], small[:, 4, 0:E]))
                c, d = 5, 1
                while d < E:
                    chain(dve.tensor_copy(small[:, 11 - c, 0:d], small[:, c, 0:d]))
                    chain(dve.tensor_tensor(small[:, 11 - c, d:E], small[:, c, d:E], small[:, c, 0:E - d], ALU.add))
                    c, d = 11 - c, 2 * d
                nj = UNITS[L]
                te = big[:, 3, 0:nj * E].rearrange("p (j e) -> p j e", e=E)
                chain(dve.tensor_tensor(te, cst[:, C_J:C_J + nj].unsqueeze(2).broadcast_to([P, nj, E]),
                                        small[:, c, 0:E].unsqueeze(1).broadcast_to([P, nj, E]), ALU.is_ge))
                chain(dve.tensor_reduce(small[:, 7, 0:nj], te, AX.X, ALU.add))
                chain(dve.tensor_scalar(tex[:, 0:nj], small[:, 7, 0:nj], float(E - 1), None, ALU.min))
                dve.sem_inc(s["tiles_ready"], 1)
                chain(dve.tensor_tensor(small[:, 11 - c, 0:E], small[:, c, 0:E], small[:, 4, 0:E], ALU.subtract))
                chain(dve.tensor_scalar(small[:, 11 - c, 0:E], small[:, 11 - c, 0:E], float(U), None, ALU.mult))
                chain(dve.tensor_tensor(v3(2), v3(a), cnt, ALU.subtract))
                chain(dve.tensor_tensor(v3(2), v3(2), rank, ALU.add))
                chain(dve.tensor_tensor(v3(2), v3(2), small[:, 11 - c, 0:E].unsqueeze(1).broadcast_to([P, KT, E]), ALU.add))
                chain(dve.tensor_tensor(v3(2), v3(2), ohb[:, 0:KT, :], ALU.mult))
                chain(dve.tensor_reduce(small[:, 7, 0:KT], v3(2), AX.X, ALU.add))
                dve.tensor_copy(pos[:, 0:KT], small[:, 7, 0:KT]).then_inc(s["pos_ready"], 1)

                def row_max(b, g, n):
                    h, qt = n // TB, n % TB
                    (wait_apart(dve, s["s_ready"], 16 * (4 * b + g) + n + 1, passed_dve) if L == 0 else
                     dve.wait_ge(s["s_ready"], 16 * (4 * b + g) + n + 1))
                    if L == 0:
                        N = (qt + 1) * P
                        dve.tensor_tensor_reduce(dump[:, n % 2, 0:N], ps[:, 4 + n % 2, 0:N], cst[:, C_MASK + 512 - N:C_MASK + 512],
                                                 1.0, -3.0e38, ALU.add, ALU.max, mx[:, g, h, qt:qt + 1]
                                                 ).then_inc(s["s_used"], 1)
                    else:
                        dve.tensor_reduce(mx[:, g, h, qt:qt + 1], ps[:, 4 + n % 2, :], AX.X, ALU.max
                                          ).then_inc(s["s_used"], 1)

                def m_lo(b, g):
                    dve.wait_ge(s["mh_ready"], NB * NG * L + 4 * b + g + 1)
                    wait(dve, s[f"min{g}"], BASE[L] + 32 * b)
                    dve.tensor_tensor(mlo[:, g, :], ps[0:G * TB, 7, 0:P], mhi[:, g, :], ALU.subtract
                                      ).then_inc(s["ml_ready"], 1)

                def normalize(b, g):
                    t = 4 * b + g
                    dve.wait_ge(s["oT_done"], t + 1)
                    oT = ps[:, 7, :].rearrange("p (q h w) -> p q h w", q=TB, h=G)
                    dve.reciprocal(rec[:, :, :], oT[:, :, :, DH]).then_inc(s["rec_ready"], 1)
                    dve.wait_ge(s["rec_ready"], t + 1)
                    dst = o_sb[:, bass.ds(b * TB, TB), g * G * DH:(g + 1) * G * DH].rearrange("p q (h d) -> p q h d", h=G)
                    dve.tensor_tensor(dst, oT[:, :, :, 0:DH], rec[:, :, :].unsqueeze(3).broadcast_to([P, TB, G, DH]),
                                      ALU.mult).then_inc(s["norm_done"], 1)

                def prev(b, g):
                    return (b, g - 1) if g else (b - 1, NG - 1)

                def slot(b, g, more, last):
                    for kt in range(TB):
                        for hp in (0, 1):
                            if more:
                                for n in range(4 * kt + 2 * hp, 4 * kt + 2 * hp + 2):
                                    row_max(b + (g + 2) // NG, (g + 2) % NG, n)
                            if (kt, hp) == (1, 1) and not last:
                                m_lo(b + (g + 1) // NG, (g + 1) % NG)
                            if (kt, hp) == (3, 0) and not (isinstance(b, int) and b == 0 and g == 0):
                                normalize(*prev(b, g))
                for g in (0, 1):
                    for n in range(16):
                        row_max(0, g, n)
                m_lo(0, 0)
                for g in range(NG):
                    slot(0, g, True, False)
                with dve.Fori(1, NB - 1) as b:
                    for g in range(NG):
                        slot(b, g, True, False)
                for g in range(NG):
                    slot(NB - 1, g, g < 2, g == NG - 1)
                normalize(NB - 1, NG - 1)

                def head(j, par):
                    dve.wait_ge(s["xeT_psum"], j + 1)
                    wait(dve, s["h_psum"], j - 1)
                    if L == 0:
                        wait_apart(dve, s[f"wu{par}"], 16 * (j // 2 + 1) if isinstance(j, int) else 16 * (half[0] + 1), passed_dve)
                        dve.tensor_scalar(xeT[:, par, :], ps[:, par, 0:U], we[:, par, W_G:W_G + 1],
                                          we[:, par, W_LB:W_LB + 1], ALU.mult, ALU.add).then_inc(s["xeT_ready"], 1)
                    else:
                        dve.tensor_copy(xeT[:, par, :], ps[:, par, 0:U]).then_inc(s["xeT_ready"], 1)

                def bias1(j, par):
                    dve.wait_ge(s["h_psum"], j + 1)
                    wait(dve, s["h_ready"], j - 1)
                    dve.tensor_tensor(hb[:, par], ps[:, 2 + 2 * par:4 + 2 * par, :].rearrange("p a (c t) -> p (a c) t", c=2),
                                      we[:, par, W_B1:W_B1 + FC].unsqueeze(2).broadcast_to([P, FC, U]), ALU.add
                                      ).then_inc(s["hb_ready"], 1)

                def bias2(j, par):
                    dve.wait_ge(s["mm2_done"], j + 1)
                    wait(dve, s[f"yo{par}"], 16 * (j // 2) if isinstance(j, int) else 16 * half[0])
                    dve.tensor_tensor(ye[:, par], ps[:, 6 + par, 0:U].rearrange("p (n d) -> p n d", n=UT),
                                      we[:, par, W_B2:W_B2 + P].unsqueeze(1).broadcast_to([P, UT, P]), ALU.add
                                      ).then_inc(s["ye_ready"], 1)
                half = [0]
                head(0, 0)
                head(1, 1)
                bias1(0, 0)

                def step(jj):
                    half[0] = jj + 1
                    head(jj * 2 + 2, 0)
                    half[0] = jj
                    bias1(jj * 2 + 1, 1)
                    bias2(jj * 2, 0)
                    half[0] = jj + 1
                    head(jj * 2 + 3, 1)
                    bias1(jj * 2 + 2, 0)
                    half[0] = jj
                    bias2(jj * 2 + 1, 1)
                each(dve, UNITS[L] // 2 - 1, step)
                n = UNITS[L] - 2
                bias1(n + 1, 1)
                bias2(n, 0)
                bias2(n + 1, 1)

                dve.wait_ge(s["gathered"], 16 * KT)

                def step(b):
                    bs = bass.ds(b * TB, TB)
                    z = zb
                    if L == 0:
                        wait(dve, s["silu_ready"], b)
                        dve.tensor_tensor(z, yg_sb[:, bs, :], xn_sb[:, bs, :], ALU.add).then_inc(s["z_ready"], 1)
                        sv = ps[:, 6, :].rearrange("p (a c) -> p a c", a=TB)
                        dve.wait_ge(s["s_psum"], b + 1)
                    else:
                        wait(dve, s["silu_ready"], b)
                        wait(dve, s["x_ready"], b)
                        w = lambda k: wch[:, k, bs].unsqueeze(2).broadcast_to([P, TB, P])
                        dve.tensor_tensor(zg, yg_sb[:, bs, :], w(0), ALU.mult).then_inc(s["chain_a"], 1)
                        dve.tensor_tensor(z, v_sb[:, bs, :], w(1), ALU.mult).then_inc(s["chain_a"], 1)
                        dve.wait_ge(s["chain_a"], NB * TB + 3 * b + 2)
                        dve.tensor_tensor(zg, zg, z, ALU.add).then_inc(s["chain_a"], 1)
                        dve.wait_ge(s["chain_a"], NB * TB + 3 * b + 3)
                        dve.tensor_tensor(z, zg, xn_sb[:, bs, :], ALU.add).then_inc(s["z_ready"], 1)
                        sv = o_sb[:, bs, :]
                    dve.wait_ge(s["silu_ready"], b + 1)
                    dve.tensor_tensor(zg, zs, sv, ALU.mult).then_inc(s["sg_ready"], 1)
                    dve.wait_ge(s["sg_ready"], b + 1)
                    dve.tensor_tensor(x_sb[:, bs, :], x_sb[:, bs, :], zg, ALU.add).then_inc(s["x_ready"], 1)
                each(dve, NB, step)
                dve.wait_ge(s["x_ready"], NB)


_INS = ["x", "rope", "const", "w0", "w1", "e0", "e1"]
_OUTS = [((8, 512, 128), 'float32')]


def layout(np, i):
    a = {k: np.asarray(v) for k, v in i.items()}
    f32 = np.float32
    r = np.arange(P)
    order = (r % H) * DH + r // H
    swapped = (r % H) * DH + ((r // H) ^ 1)
    wq, wk = a["L0_attn_wq"], a["L0_attn_wk"]
    w0 = np.concatenate([wq[order].T, wq[swapped].T, wk[order].T, wk[swapped].T, a["L0_attn_wv"].T, a["L0_attn_wo"].T,
                         a["L0_ffn_centroids"].T], axis=1)
    chunks = lambda w: w.reshape(FC, P, P).transpose(1, 0, 2).reshape(P, F)
    everywhere = lambda v: np.broadcast_to(v[None, :], (P, P))
    w1 = np.concatenate([a["L1_attn_Wq"][:, order], a["L1_attn_Wk"][:, order], a["L1_attn_Wk"], a["L1_ffn_gate_w"].T,
                         a["L1_ffn_sw_in"], chunks(a["L1_ffn_sw_out"]), a["L1_attn_bq"][order][:, None],
                         a["L1_attn_bk"][order][:, None], everywhere(a["L1_attn_bk"]),
                         a["L1_ffn_sb_in"].reshape(FC, P).T, everywhere(a["L1_ffn_sb_out"])], axis=1)

    def experts(W1, W2, b1, b2, *more):
        return np.ascontiguousarray(np.stack([np.concatenate(
            [chunks(W2[e]), everywhere(b2[e]), W1[e], b1[e].reshape(FC, P).T] + [m[e][:, None] for m in more], axis=1)
            for e in range(E)]))
    e0 = experts(a["L0_ffn_W1"], a["L0_ffn_W2"], a["L0_ffn_b1"], a["L0_ffn_b2"], a["L0_ffn_ln_g"], a["L0_ffn_ln_b"])
    e1 = experts(a["L1_ffn_w_in"], a["L1_ffn_w_out"], a["L1_ffn_b_in"], a["L1_ffn_b_out"])
    d = r // H
    freq = (f32(1.0) / f32(10000.0) ** (np.arange(0, DH, 2, dtype=f32) / f32(DH))).astype(f32)
    ang = np.outer(freq[d // 2], np.arange(TB * P, dtype=f32)).astype(f32)
    rope = np.stack([np.cos(ang), np.where(d % 2 == 0, -1, 1)[:, None] * np.sin(ang)], axis=1).astype(f32)
    const = np.zeros((P, NCONST), f32)
    const[:, C_ID:C_ID + P] = np.eye(P)
    const[:, C_UP:C_UP + P] = r[:, None] < r[None, :]
    const[:, C_ONE:C_ONE + P] = 1
    const[:, C_MASK + 384:C_MASK + 512] = np.where(r[None, :] > r[:, None], -BIG, 0)
    const[:, C_DESC:C_DESC + E] = E - np.arange(E)
    const[:, C_JU:C_JU + UE] = U * np.arange(UE)
    const[:, C_J:C_J + UNITS[1]] = np.arange(UNITS[1])
    const[:, C_NHALF:C_NHALF + TB] = -0.5
    return [a["L0_attn_x"], rope, const, w0, w1, e0, e1]


def kernel(**inputs):
    import numpy as _np
    import concourse.bacc as _bacc
    from concourse import mybir as _mybir
    from concourse.bass_utils import run_bass_kernel_spmd as _run

    nc = _bacc.Bacc("TRN2", target_bir_lowering=False, num_devices=1)
    arrays, args = {}, []
    for name, a in zip(_INS, layout(_np, inputs)):
        a = _np.ascontiguousarray(a)
        arrays[f"in_{name}_dram"] = a
        args.append(nc.dram_tensor(f"in_{name}_dram", a.shape, _mybir.dt.from_np(a.dtype), kind="ExternalInput").ap())
    for i, (shape, dtype) in enumerate(_OUTS):
        dt = _mybir.dt.from_np(_np.dtype(dtype))
        args.append(nc.dram_tensor(f"out_{i}_dram", shape, dt, kind="ExternalOutput").ap())
    build(nc, *args)
    r = _run(nc, [arrays], core_ids=[0])
    got = tuple(r.results[0][f"out_{i}_dram"] for i in range(len(_OUTS)))
    return got[0]
```

```python
from contextlib import ExitStack

import numpy as np

import concourse.bass as bass
from concourse import mybir

F32 = mybir.dt.float32
BF16 = mybir.dt.bfloat16
U32 = mybir.dt.uint32
I32 = mybir.dt.int32
ALU = mybir.AluOpType
ACT = mybir.ActivationFunctionType
AX = mybir.AxisListType

P = 128
NB = 8
TB = 4
NT = NB * TB
H = 16
DH = 8
E = 8
F = 512
FC = F // P
G = 4
NG = H // G
VW = 32
KS = 48
KM = 50
EPS = 1e-5
BIG = 1e30
CHOICES = (1, 2)
U = 256
UT = U // P
UNITS = tuple(k * NB * TB * P // U + E - 1 for k in CHOICES)
SCALE = (DH ** -0.5, P ** -0.5)
PLACES = (((0, 1, 3), (3, 2, 2), (4, 1, 1)),
          ((2, 1, 3), (1, 4, 2), (0, 1, 1)))
STEPS = ([(kt, [h]) for kt in (0, 1) for h in range(4)] + [(2, [0, 1]), (2, [2, 3]), (3, [0, 1, 2, 3])],
         [(kt, [h]) for kt in range(4) for h in range(4)])
SUMS = ({0: (2, True), 2: (3, True), 6: (0, False), 9: (1, False)},
        {2: (3, True), 6: (0, False), 10: (1, False), 14: (2, False)})
O_COPY = (4, 2)
O_TURN = (8, 8)
M_TURN = (3, 3)
M_SPLIT = (4, 4)
O_NORM = (9, 10)
GATE = ((4, 7, 10), (4, 9, 14))
ITEMS = (16, 8)
HALF = NB // 2

C_ID, C_UP, C_ONE, C_MASK = 0, 128, 256, 384
C_DESC, C_JU, C_J, C_NHALF, C_MASKT = 896, 904, 920, 960, 992
NCONST = 992 + 128
UE = NT * P // U
W_2, W_B2, W_1 = 0, F, F + P
W_B1, W_G, W_LB = W_1 + F, W_1 + F + FC, W_1 + F + FC + 1
NW = (W_LB + 1, W_G)


def wait(eng, sem, value):
    if isinstance(value, int) and value <= 0:
        return
    eng.wait_ge(sem, value)


def each(eng, n, body):
    body(0)
    with eng.Fori(1, n) as i:
        body(i)


def in_pairs(eng, first, second, last):
    first(0, 0)

    def pair(k):
        for i in (1, 2):
            b = k * 2 + i
            first(b, i % 2)
            second(b - 1, 1 - i % 2)
    each(eng, NB // 2 - 1, pair)
    last()
    second(NB - 2, 0)
    second(NB - 1, 1)


def shared_banks(b):
    return (2, 3, 4) if isinstance(b, int) and b == NB - 1 else (1, 3, 6)


def parts_out(b, par):
    return 48 * (b - par)


def wait_apart(eng, sem, value, passed):
    eng.wait_ge(sem, value)
    if not isinstance(value, int):
        eng.sem_inc(passed, 1)


def build(nc, x_in, rope_in, const_in, w0_in, w1_in, e0_in, e1_in, out):
    ctx = ExitStack()
    with ctx:
        def sb(name, shape, dt=F32):
            return ctx.enter_context(nc.sbuf_tensor(name, shape, dt))

        def pb(name, shape, dt=F32):
            return ctx.enter_context(nc.psum_tensor(name, shape, dt))

        def sem(name):
            return ctx.enter_context(nc.semaphore(name))

        def dram(name, shape, dt):
            return nc.dram_tensor(name, shape, dt, kind="Internal").ap()

        epack = (e0_in, e1_in)
        qk_d = [dram(f"qk_d{L}", [2, NB, 6 * DH, H, TB * P], BF16) for L in (0, 1)]
        xs_d = [dram(f"xs_d{L}", [UNITS[L] * U, P], F32) for L in (0, 1)]
        ys_d = [dram(f"ys_d{L}", [UNITS[L] * U, P], F32) for L in (0, 1)]

        zq_d = dram("zq_d", [2, G, TB * P], BF16)

        cst = sb("cst", [P, NCONST])
        rope = sb("rope", [P, 2, TB * P])
        w0 = sb("w0", [P, 6 * P + E])
        w1 = sb("w1", [P, 3 * P + E + 2 * F + 2 + P + FC + P])
        idb = cst[:, C_ID:C_ID + P]
        upb = sb("upb", [P, P], BF16)
        oneb = sb("oneb", [P, P], BF16)
        idbf = sb("idbf", [P, P], BF16)
        maskb = sb("maskb", [P, P], BF16)
        x_sb = sb("x_sb", [P, NT, P])
        xn_sb = sb("xn_sb", [P, NT, P])
        xs_sb = sb("xs_sb", [P, NT, P])
        v_sb = sb("v_sb", [P, NT, P])
        o_sb = sb("o_sb", [P, NT, P])
        yg_sb = sb("yg_sb", [P, NT, P])
        v2_sb = xs_sb
        temps = [t[:, :, :].rearrange("p a b -> p (a b)").rearrange("p (k s t) -> p k s t", k=4, s=2)
                 for t in (yg_sb, o_sb)]
        cosq, sinq, qf, r1 = ([t[:, k] for t in temps] for k in range(4))
        parts0 = [sb(f"part{k}", [P, 2, TB * P], BF16) for k in range(3)]
        st6 = sb("st6", [P, NT, 6])
        mv = sb("mv", [P, NT, 2])
        rstd = sb("rstd", [P, 2, NT])
        vare = sb("vare", [P, 3, NT])
        xns0 = sb("xns", [P, TB, P])
        xT = sb("xT", [P, TB * P])
        xe = sb("xe", [P, 2, UT, P])
        lg = sb("lg", [P, NT, E])
        Qs = sb("Qs", [P, NG, G, TB * P], BF16)
        Ks = sb("Ks", [P, NG, G, TB * P], BF16)
        PT = sb("PT", [P, 2, G, TB * P])
        parts = [[t[:, :, :] for t in parts0],
                 [PT[:, 1, 1 + k, :].bitcast(BF16).rearrange("p (s t) -> p s t", s=2) for k in range(3)]]
        xTs = xT[:, :], PT[:, 1, 0, :]
        hsh = PT[:, :, :, :]
        Vs = sb("Vs", [P, NG, TB, G, VW])
        neg1 = float(np.array([0xBF80BF80], np.uint32).view(np.float32)[0])
        mx = sb("mx", [P, NG, G, TB])
        mhi = sb("mhi", [G * TB, NG, P], BF16)
        mlo = sb("mlo", [G * TB, NG, P], BF16)
        dump = sb("dump", [P, P * TB * (TB + 1) // 2], BF16)
        oc = xT
        rec = sb("rec", [P, TB, G])
        oT = xns0[:, :, :].rearrange("p a c -> p (a c)"), xe[:, :, :, :].rearrange("p a n d -> p (a n d)")
        small = sb("small", [P, 8, 2 * NT])
        ohb = sb("ohb", [P, 2 * NT, E], BF16)
        pos = sb("pos", [P, 2 * NT], U32)
        tex = sb("tex", [P, UNITS[1]], I32)
        wch = sb("wch", [P, 2, NT])
        zero = sb("zero", [P, P])
        we = sb("we", [P, 2, NW[0]])
        big = we[:, :, :].rearrange("p a n -> p (a n)")[:, 0:4 * 512].rearrange("p (k t) -> p k t", k=4)
        xeT = sb("xeT", [P, 2, U])
        flat = PT[:, :, :, :].rearrange("p k h t -> p (k h t)").rearrange("p (k r c u) -> p k r c u", k=2, r=2, c=FC)
        hb, hT = flat[:, 0], flat[:, 1]
        ye = sb("ye", [P, 2, UT, P])
        xns = xns0[:, :, :], xe[:, :, :, :].rearrange("p a n d -> p (a n) d")
        xn2s = [PT[:, 0, k, :].rearrange("p (a c) -> p a c", a=TB) for k in (0, 1)]

        ps = pb("ps", [P, 8, 512])

        s_x = sem("x_loaded")
        s_load = sem("inputs_loaded")
        s_rest = sem("rest_loaded")
        s_w1 = sem("w1_loaded")
        s_stats = sem("x_stats")
        s_rstd = sem("rstd_ready")
        s_setup = sem("setup_done")
        S = []
        LOADS = {n: sem(n) for n in "ld0 ld1 ld2 ld3 min0 min1 min2 min3 mT_ready mh_ready ml_ready".split()}
        BASE = (0, 32 * NB)
        for L in (0, 1):
            names = """chain_v chain_g xm_ready xn_ready xn2_ready xn_saved0 xn_saved1 xT_psum xT_ready
                mm_q0 mm_q1 mm_v mm_lg rope_q0 rope_q1 qf_0 qf_1 p1_0 p1_1 r1_0 r1_1 p2_0 p2_1 p3_0 p3_1 out_0 out_1
                v_saved lg_saved rec_ready sh_psum sh_h sh_y sh_saved
                onehot_ready counts_ready pos_ready gate_exp zeroed scattered tiles_ready
                ld0 ld1 ld2 ld3 min0 min1 min2 min3 s_ready s_used mT_ready mh_ready ml_ready st_ready exp_done pv_done
                o_copied oT_done norm_done v_ready
                wu0 wu1 wd0 wd1 xe0 xe1 xeT_psum xeT_ready h_psum hb_ready h_ready mm2_done ye_ready yo0 yo1 gathered
                oT2_psum oT2_ready s_psum z_part z_ready silu_ready sg_ready x_ready""".split()
            unused = ("z_part sh_psum sh_h sh_y sh_saved gate_exp", "xn2_ready rope_q0 rope_q1 oT2_psum oT2_ready s_psum")
            S.append({n: sem(f"{n}_{L}") for n in names if n not in unused[L].split() and n not in LOADS})
            S[L].update(LOADS)
        s_stat = sem("statistics")
        s_out = sem("out_stored")
        passed_dve = sem("passed_dve")
        block = ctx.enter_context(nc.Block())

        rows = lambda ap: ap.rearrange("(n p) d -> p n d", p=P)

        def first_query(L, kt):
            return kt * P if L == 0 else 0

        @block.sync
        def _(sp):
            xr = x_in.rearrange("b (n p) d -> p (b n) d", p=P)
            sp.dma_start(x_sb[:, 0:8, :], xr[:, 0:8, :]).then_inc(s_x, 16)
            sp.dma_start(cst[:, :], const_in).then_inc(s_load, 16)
            sp.dma_start(w0[:, :], w0_in).then_inc(s_load, 16)
            for n in range(8, NT, 8):
                sp.dma_start(x_sb[:, n:n + 8, :], xr[:, n:n + 8, :]).then_inc(s_rest, 16)
            sp.dma_start(rope[:, :, :], rope_in).then_inc(s_rest, 16)
            sp.dma_start(w1[:, :], w1_in).then_inc(s_w1, 16)
            sp.wait_ge(s_setup, 2)
            sp.dma_start(zq_d, Qs[KS:KM, 0, :, :]).then_inc(s_setup, 16)
            sp.wait_ge(s_setup, 2 + 16)
            for L in (0, 1):
                s = S[L]
                for j in range(0, UNITS[L] * UT, 8):
                    n = min(8, UNITS[L] * UT - j)
                    sp.dma_start(rows(xs_d[L])[:, j:j + n, :], zero[:, :].unsqueeze(1).broadcast_to([P, n, P])
                                 ).then_inc(s["zeroed"], 16)

                def save_rows(b, par):
                    at = bass.ds(sp.snap(b * TB), TB)
                    sp.wait_ge(s["xn_ready"], b + 1)
                    if L == 0:
                        sp.wait_ge(s["xn2_ready"], b + 1)
                        sp.dma_start(xn_sb[:, at, :], xns[par]).then_inc(s[f"xn_saved{par}"], 16)
                        sp.dma_start(xs_sb[:, at, :], xn2s[par]).then_inc(s[f"xn_saved{par}"], 16)
                    else:
                        sp.dma_start(xs_sb[:, at, :], xns[par]).then_inc(s[f"xn_saved{par}"], 16)

                def save_parts(b, par):
                    for i in (0, 1):
                        dst = qk_d[L][i, bass.ds(b, 1)].rearrange("o (c d) h t -> (o d h) c t", c=6)
                        for k in range(3):
                            sp.wait_ge(s[f"p{k + 1}_{i}"], b + 1)
                            first, by, n = PLACES[i][k]
                            src = parts[par][k][:, i, :].unsqueeze(1).broadcast_to([P, n, TB * P])
                            sp.dma_start(dst[:, first:first + by * (n - 1) + 1:by, :], src).then_inc(s[f"out_{par}"], 16)
                last_exp = len(STEPS[L])

                def load(b, g):
                    wait(sp, s["exp_done"], last_exp * (4 * b + g - 3))
                    bb = bass.ds(b, 1)
                    for dstk, i in ((Qs, 0), (Ks, 1)):
                        src = qk_d[L][i, bb, :, g * G:(g + 1) * G, :].rearrange("o r h t -> (o r) h t")
                        sp.dma_start(dstk[0:KS, g, :, :], src).then_inc(s[f"ld{g}"], 16)
                    sp.dma_start(Qs[KS:KM, g, :, :], zq_d).then_inc(s[f"ld{g}"], 16)

                def last():
                    save_rows(NB - 1, 1)
                    for g in range(NG):
                        load(0, g)
                in_pairs(sp, save_rows, save_parts, last)
                for par in (0, 1):
                    sp.wait_ge(s[f"out_{par}"], 16 * 6 * NB // 2)

                def maxima(b, g):
                    sp.wait_ge(s["ml_ready"], NB * NG * L + 4 * b + g + 1)
                    for r, m in ((KS, mhi), (KS + 1, mlo)):
                        dst = Qs[r:r + 1, g, :, :].rearrange("o h (q t) -> o (h q) t", t=P)
                        sp.dma_start(dst, m[:, g, :]).then_inc(s[f"min{g}"], 16)

                def attention(b0):
                    def batch(b):
                        for g in range(NG):
                            if not (isinstance(b, int) and b == NB - 1):
                                maxima(b + (g + 1) // NG, (g + 1) % NG)
                                if not (isinstance(b, int) and b == HALF - 1 and g == NG - 1):
                                    load(b + 1, g)
                            elif g < NG - 1:
                                maxima(b, g + 1)
                    batch(b0)
                    with sp.Fori(b0 + 1, b0 + HALF - 1) as b:
                        batch(b)
                    batch(b0 + HALF - 1)
                maxima(0, 0)
                attention(0)
                sp.wait_ge(s["tiles_ready"], 1)
                sp.wait_ge(s["scattered"], 16 * CHOICES[L] * NT)
                units = lambda ap: ap.rearrange("(j n p) d -> j p n d", p=P, n=UT)

                def expert(j, lo, hi):
                    e = sp.value_load(tex[0:1, bass.ds(j, 1)], min_val=0, max_val=E - 1)
                    return epack[L][bass.ds(e, 1), :, lo:hi].rearrange("o p n -> (o p) n")

                def feed_rows(j, par):
                    wait(sp, s["xeT_psum"], j - 1)
                    sp.dma_start(xe[:, par, :, :], units(xs_d[L])[bass.ds(j, 1)].rearrange("o p n d -> (o p) n d")
                                 ).then_inc(s[f"xe{par}"], 16)

                def feed_up(j, par):
                    src = expert(j, W_1, NW[L])
                    wait(sp, s["hb_ready"], j - 1)
                    sp.dma_start(we[:, par, W_1:NW[L]], src).then_inc(s[f"wu{par}"], 16)

                def feed_down(j, par):
                    src = expert(j, 0, W_1)
                    wait(sp, s["ye_ready"], j - 1)
                    sp.dma_start(we[:, par, 0:W_1], src).then_inc(s[f"wd{par}"], 16)

                def drain(j, par):
                    sp.wait_ge(s["ye_ready"], j + 1)
                    sp.dma_start(units(ys_d[L])[bass.ds(j, 1)].rearrange("o p n d -> (o p) n d"), ye[:, par, :, :]
                                 ).then_inc(s[f"yo{par}"], 16)

                for j in (0, 1):
                    feed_rows(j, j)
                    feed_up(j, j)
                    feed_down(j, j)
                load(HALF, NG - 1)
                feed_rows(2, 0)
                feed_rows(3, 1)
                feed_up(2, 0)

                def step(jj):
                    for par in (0, 1):
                        feed_rows(jj * 2 + par + 4, par)
                        feed_up(jj * 2 + par + 3, 1 - par)
                        feed_down(jj * 2 + par + 2, par)
                        drain(jj * 2 + par, par)
                each(sp, UNITS[L] // 2 - 2, step)
                n = UNITS[L] - 1
                feed_rows(n, 0)
                feed_up(n - 1, 1)
                feed_down(n - 2, 0)
                drain(n - 4, 0)
                feed_up(n, 0)
                feed_down(n - 1, 1)
                drain(n - 3, 1)
                feed_down(n, 0)
                for j in (n - 2, n - 1, n):
                    drain(j, j % 2)
                attention(HALF)
                if L == 1:
                    outr = out.rearrange("b (n p) d -> p (b n) d", p=P)
                    for b in range(NB):
                        sp.wait_ge(s["x_ready"], b + 1)
                        sp.dma_start(outr[:, b * TB:(b + 1) * TB, :], x_sb[:, b * TB:(b + 1) * TB, :]).then_inc(s_out, 16)
                    sp.wait_ge(s_out, 16 * NB)

        @block.gpsimd
        def _(pool):
            pool.memset(zero[:, :], 0.0).then_inc(s_setup, 1)
            for L in (0, 1):
                s = S[L]
                links = [0]

                def chain(ins):
                    links[0] += 1
                    ins.then_inc(s["chain_g"], 1)
                    pool.wait_ge(s["chain_g"], links[0])
                if L == 0:
                    chain(pool.memset(Vs[:, :, :, :, :], 0.0))
                    chain(pool.memset(Qs[:, :, :, :].rearrange("p g h t -> p (g h t)").bitcast(F32), 0.0))
                    pool.memset(Vs[:, :, :, :, DH:DH + 1].rearrange("p g k h o -> p (g k h) o"), 1.0).then_inc(s_setup, 1)
                    pool.wait_ge(s_load, 16 * 2)
                nhalf = cst[:, C_NHALF:C_NHALF + NT]

                def rstd_of(first, end, stats_seen):
                    at = slice(first, end)
                    pool.wait_ge(s_stats, stats_seen)
                    chain(pool.tensor_scalar(vare[:, 0, at], mv[:, at, 1], EPS, None, ALU.add))
                    if L == 1:
                        pool.tensor_tensor(rstd[:, 0, at], vare[:, 0, at], nhalf[:, at], ALU.pow).then_inc(s_rstd, 1)
                    else:
                        chain(pool.tensor_tensor(rstd[:, 0, at], vare[:, 0, at], nhalf[:, at], ALU.pow))
                        chain(pool.tensor_tensor(vare[:, 1, at], mv[:, at, 1], rstd[:, 0, at], ALU.mult))
                        chain(pool.tensor_tensor(vare[:, 2, at], vare[:, 1, at], rstd[:, 0, at], ALU.mult))
                        chain(pool.tensor_scalar(vare[:, 1, at], vare[:, 2, at], EPS, None, ALU.add))
                        pool.tensor_tensor(rstd[:, 1, at], vare[:, 1, at], nhalf[:, at], ALU.pow).then_inc(s_rstd, 1)

                if L == 0:
                    rstd_of(0, 8, 1)
                    rstd_of(8, 16, 2)
                else:
                    for n in range(0, NT, 8):
                        rstd_of(n, n + 8, 2 + (n + 8) // TB)

                def rotated(b, par):
                    if L == 0:
                        for i in (0, 1):
                            pool.wait_ge(s[f"rope_q{i}"], b + 1)
                            wait(pool, s[f"p3_{i}"], b - 1)
                            wait(pool, s[f"r1_{i}"], b - 1)
                            pool.tensor_tensor(qf[par][:, i, :], cosq[par][:, i, :], sinq[par][:, i, :], ALU.add
                                               ).then_inc(s[f"qf_{i}"], 1)
                        if isinstance(b, int) and b == 0:
                            rstd_of(16, NT, 2)

                def third_part(b, par):
                    for i in (0, 1):
                        pool.wait_ge(s[f"p2_{i}"], b + 1)
                        wait(pool, s[f"out_{par}"], parts_out(b, par))
                        pool.tensor_tensor(parts[par][2][:, i, :], r1[par][:, i, :], parts[par][1][:, i, :], ALU.subtract
                                           ).then_inc(s[f"p3_{i}"], 1)
                in_pairs(pool, rotated, third_part, lambda: rotated(NB - 1, 1))
                pool.wait_ge(s["pos_ready"], 1)
                pool.wait_ge(s["zeroed"], 16 * -(-UNITS[L] * UT // 8))
                for par in (0, 1):
                    pool.wait_ge(s[f"xn_saved{par}"], 16 * NB // 2 * (2 if L == 0 else 1))

                def scatter(n):
                    pool.indirect_dma_start(xs_d[L], bass.IndirectOffsetOnAxis(ap=pos[:, n:n + 1], axis=0),
                                            xs_sb[:, n % NT, :], None).then_inc(s["scattered"], 16)

                n_steps = len(STEPS[L])

                def v_slot(b, g):
                    if not isinstance(b, int) or b:
                        wait_apart(pool, s["pv_done"], 4 * (4 * b + g - 4) + 4, passed_dve)
                    src = v_sb[:, bass.ds(b * TB, TB), g * G * DH:(g + 1) * G * DH].rearrange(
                        "p k (h d) -> p k h d", h=G)
                    pool.tensor_copy(Vs[:, g, :, :, 0:DH], src).then_inc(s["v_ready"], 1)

                def v_slots(b, final):
                    for g in range(NG):
                        if not (final and g >= 2):
                            v_slot(b + (g + 2) // NG, (g + 2) % NG)
                        yield g

                def add_shared(k):
                    at = bass.ds(pool.snap(k * TB), TB)
                    z = yg_sb[:, at, :]
                    if L == 1:
                        for c, rows_ in enumerate((z, v2_sb[:, at, :])):
                            pool.tensor_tensor(rows_, rows_, wch[:, c, at].unsqueeze(2).broadcast_to([P, TB, P]), ALU.mult
                                               ).then_inc(s["z_part"], 1)
                        wait_apart(pool, s["z_part"], 3 * k + 2, passed_dve)
                        pool.tensor_tensor(z, z, v2_sb[:, at, :], ALU.add).then_inc(s["z_part"], 1)
                        wait_apart(pool, s["z_part"], 3 * k + 3, passed_dve)
                    pool.tensor_tensor(z, z, xn_sb[:, at, :], ALU.add).then_inc(s["z_ready"], 1)

                def gather(n):
                    dst = (yg_sb if n < NT else v2_sb)[:, n % NT, :]
                    pool.indirect_dma_start(dst, None, ys_d[L],
                                            bass.IndirectOffsetOnAxis(ap=pos[:, n:n + 1], axis=0)
                                            ).then_inc(s["gathered"], 16)
                pool.wait_ge(s["v_saved"], NB)
                share = CHOICES[L] * NT // NG
                v_slot(0, 0)
                v_slot(0, 1)
                for g in v_slots(0, False):
                    for n in range(g * share, (g + 1) * share):
                        scatter(n)
                with pool.Fori(1, HALF - 1) as b:
                    for g in v_slots(b, False):
                        pass
                for g in v_slots(HALF - 1, False):
                    pass
                for par in (0, 1):
                    pool.wait_ge(s[f"yo{par}"], 16 * ((UNITS[L] + 1 - par) // 2))
                for g in v_slots(HALF, False):
                    for n in range(g * share, (g + 1) * share):
                        gather(n)
                pool.wait_ge(s["gathered"], 16 * CHOICES[L] * NT)
                with pool.Fori(HALF + 1, NB - 1) as b:
                    for g in v_slots(b, False):
                        add_shared((b - HALF - 1) * NG + g)
                for g in v_slots(NB - 1, True):
                    pass
                if L == 0:
                    for b in range(NB):
                        at = slice(b * TB, (b + 1) * TB)
                        pool.wait_ge(s["sg_ready"], b + 1)
                        pool.tensor_tensor(x_sb[:, at, :], x_sb[:, at, :], yg_sb[:, at, :], ALU.add).then_inc(s["x_ready"], 1)

        @block.scalar
        def _(act):
            for L in (0, 1):
                s = S[L]
                if L == 1:
                    act.wait_ge(s_w1, 16)

                C_SBIN = 3 * P + E + 2 * F + 2 + P

                def x_T(b, par):
                    act.wait_ge(s["xT_psum"], b + 1)
                    wait(act, s["mm_lg"] if L == 0 else s["sh_psum"], b - 1 if L == 0 else FC * (b - 1))
                    act.copy(xTs[par], ps[:, 7, :]).then_inc(s["xT_ready"], 1)

                def first_part(b, par):
                    if L == 1:
                        for i in (0, 1):
                            act.wait_ge(s[f"mm_q{i}"], b + 1)
                            wait(act, s[f"p3_{i}"], b - 1)
                            wait(act, s[f"r1_{i}"], b - 1)
                            act.activation(qf[par][:, i, :], ps[:, 2 * i, :], ACT.Identity,
                                           bias=w1[:, 3 * P + E + 2 * F + i:3 * P + E + 2 * F + i + 1]
                                           ).then_inc(s[f"qf_{i}"], 1)
                    for i in (0, 1):
                        act.wait_ge(s[f"qf_{i}"], b + 1)
                        wait(act, s[f"out_{par}"], parts_out(b, par))
                        act.copy(parts[par][0][:, i, :], qf[par][:, i, :]).then_inc(s[f"p1_{i}"], 1)

                def rest(b, par):
                    if L == 0:
                        act.wait_ge(s["mm_v"], b + 1)
                        act.copy(v_sb[:, bass.ds(b * TB, TB), :],
                                 ps[:, 4, :].rearrange("p (a c) -> p a c", a=TB)).then_inc(s["v_saved"], 1)
                    elif not (isinstance(b, int) and b == 0):
                        shared_act(b - 1)

                def shared_act(b):
                    for c in range(FC):
                        act.wait_ge(s["sh_psum"], FC * b + c + 1)
                        wait(act, s["sh_y"], b)
                        act.activation(hsh[:, 0, c, :], ps[:, shared_banks(b)[c % 2], :], ACT.Gelu,
                                       bias=w1[:, C_SBIN + c:C_SBIN + c + 1]).then_inc(s["sh_h"], 1)

                def second_part(b, par):
                    for i in (0, 1):
                        act.wait_ge(s[f"r1_{i}"], b + 1)
                        act.copy(parts[par][1][:, i, :], r1[par][:, i, :]).then_inc(s[f"p2_{i}"], 1)

                def stage(b, par):
                    if L == 0:
                        rest(b, par)
                        x_T(b + 1, 1 - par)
                        first_part(b, par)
                    else:
                        first_part(b, par)
                        rest(b, par)
                        x_T(b + 1, 1 - par)

                def last():
                    first_part(NB - 1, 1)
                    rest(NB - 1, 1)
                x_T(0, 0)
                in_pairs(act, stage, second_part, last)
                if L == 1:
                    shared_act(NB - 1)

                n_steps = len(STEPS[L])

                def m_hi(b, g):
                    act.wait_ge(s["mT_ready"], NB * NG * L + 4 * b + g + 1)
                    wait(act, s[f"min{g}"], BASE[L] + 32 * b)
                    act.copy(mhi[:, g, :], ps[0:G * TB, 7, 0:P]).then_inc(s["mh_ready"], 1)

                def o_copy(b, g):
                    act.wait_ge(s["pv_done"], 4 * (4 * b + g) + 4)
                    wait(act, s["oT_done"], 4 * b + g)
                    act.copy(oc[:, :], ps[:, 6, :]).then_inc(s["o_copied"], 1)

                def prev(b, g):
                    return (b, g - 1) if g else (b - 1, NG - 1)

                def gates():
                    act.wait_ge(s["z_ready"], NB)
                    for c in range(0, NT, 8):
                        z = yg_sb[:, c:c + 8, :]
                        act.activation(z, z, ACT.Silu).then_inc(s["silu_ready"], 1)

                def copy_oT(b):
                    act.wait_ge(s["oT2_psum"], b + 1)
                    wait(act, s["s_psum"], b - 1)
                    act.copy(oT[b % 2], ps[:, 2 + b % 2, :]).then_inc(s["oT2_ready"], 1)

                def attention(b0):
                    def batch(b):
                        for g in range(NG):
                            t = 4 * b + g
                            first = isinstance(b, int) and b == b0 and g == 0
                            last = isinstance(b, int) and b == NB - 1 and g == NG - 1
                            for i, (kt, hs) in enumerate(STEPS[L]):
                                act.wait_ge(s["st_ready"], n_steps * t + i + 1)
                                wait(act, s["pv_done"], 4 * t + kt - 1)
                                q0 = first_query(L, kt)
                                src = ps[:, (n_steps * g + i) % 2, 0:len(hs) * (512 - q0)].rearrange(
                                    "p (h t) -> p h t", h=len(hs))
                                act.activation(PT[:, kt % 2, hs[0]:hs[-1] + 1, q0:], src, ACT.Exp, scale=SCALE[L]
                                               ).then_inc(s["exp_done"], 1)
                                if i == O_COPY[L] and not first:
                                    o_copy(*prev(b, g))
                                if i == M_TURN[L] and not last:
                                    m_hi(b + (g + 1) // NG, (g + 1) % NG)
                                if isinstance(b, int) and b == NB - 1 and g >= 2:
                                    if g == 2 and i == 0:
                                        gates()
                                    if L == 0 and i + 3 in GATE[L]:
                                        copy_oT((g - 2) * len(GATE[L]) + GATE[L].index(i + 3))
                    batch(b0)
                    with act.Fori(b0 + 1, b0 + HALF - 1) as b:
                        batch(b)
                    batch(b0 + HALF - 1)
                    o_copy(b0 + HALF - 1, NG - 1)
                m_hi(0, 0)
                attention(0)

                if L == 1:
                    act.wait_ge(s["gate_exp"], 1)
                    act.activation(lg[:, :, :], lg[:, :, :], ACT.Exp).then_inc(s["gate_exp"], 1)
                    act.wait_ge(s["gate_exp"], 3)
                    act.activation(small[:, 2, 0:NT], small[:, 2, 0:NT], ACT.Exp).then_inc(s["gate_exp"], 1)

                def hidden(j, par):
                    act.wait_ge(s["hb_ready"], j + 1)
                    wait(act, s["mm2_done"], j - 1)
                    act.activation(hT[:, par].rearrange("p c t -> p (c t)"), hb[:, par].rearrange("p c t -> p (c t)"),
                                   ACT.Relu if L == 0 else ACT.Gelu).then_inc(s["h_ready"], 1)

                def step(jj):
                    hidden(jj * 2, 0)
                    hidden(jj * 2 + 1, 1)
                each(act, UNITS[L] // 2, step)
                hidden(UNITS[L] - 1, 0)

                attention(HALF)
                if L == 0:
                    for b in range(2 * len(GATE[L]), NB):
                        copy_oT(b)

        @block.tensor
        def _(pe):
            pe.wait_ge(s_load, 16 * 2)
            for L in (0, 1):
                s = S[L]
                if L == 1:
                    pe.wait_ge(s_w1, 16)

                def x_T(b, par):
                    pe.wait_ge(s["xn_ready"], b + 1)
                    wait(pe, s["xT_ready"], b)
                    for n in range(TB):
                        mm = pe.transpose(ps[:, 7, n * P:(n + 1) * P], xns[par][:, n, :], idb)
                    mm.then_inc(s["xT_psum"], 1)

                def proj(b, par):
                    xT = xTs[par]
                    pe.wait_ge(s["xT_ready"], b + 1)
                    w = w0 if L == 0 else w1
                    for i in (0, 1):
                        if L == 0:
                            wait(pe, s[f"rope_q{i}"], b)
                            pe.matmul(ps[:, 2 * i, :], w[:, 2 * i * P:(2 * i + 1) * P], xT, start=True, stop=True)
                            mm = pe.matmul(ps[:, 2 * i + 1, :], w[:, (2 * i + 1) * P:(2 * i + 2) * P], xT,
                                           start=True, stop=True)
                        else:
                            wait(pe, s[f"qf_{i}"], b)
                            mm = pe.matmul(ps[:, 2 * i, :], w[:, i * P:(i + 1) * P], xT, start=True, stop=True)
                        mm.then_inc(s[f"mm_q{i}"], 1)
                    wait(pe, s["v_saved"], b)
                    wv = w0[:, 4 * P:5 * P] if L == 0 else w1[:, 2 * P:3 * P]
                    for n in range(TB):
                        mm = pe.matmul(ps[:, 4, n * P:(n + 1) * P], xT[:, n * P:(n + 1) * P], wv, start=True, stop=True)
                    mm.then_inc(s["mm_v"], 1)
                    wait(pe, s["lg_saved"], b)
                    wr = w0[:, 6 * P:6 * P + E] if L == 0 else w1[:, 3 * P:3 * P + E]
                    for n in range(TB):
                        mm = pe.matmul(ps[:, 5, n * E:(n + 1) * E], xT[:, n * P:(n + 1) * P], wr, start=True, stop=True)
                    mm.then_inc(s["mm_lg"], 1)

                def shared_up(b, par):
                    sw = 3 * P + E
                    for c in range(FC):
                        wait(pe, s["sh_h"], FC * b + (c - 1 if c >= 2 else 0))
                        mm = pe.matmul(ps[:, shared_banks(b)[c % 2], :], w1[:, sw + c * P:sw + (c + 1) * P], xTs[par],
                                       start=True, stop=True)
                        mm.then_inc(s["sh_psum"], 1)

                def shared_down(b):
                    pe.wait_ge(s["sh_h"], FC * b + FC)
                    if not (isinstance(b, int) and b == NB - 1):
                        wait(pe, s["sh_saved"], b)
                    sw = 3 * P + E + F
                    for n in range(TB):
                        for c in range(FC):
                            mm = pe.matmul(ps[:, shared_banks(b)[2], n * P:(n + 1) * P], hsh[:, 0, c, n * P:(n + 1) * P],
                                           w1[:, sw + c * P:sw + (c + 1) * P], start=(c == 0), stop=(c == FC - 1))
                    mm.then_inc(s["sh_y"], 1)

                def stage(b, par):
                    proj(b, par)
                    behind = L == 1 and not (isinstance(b, int) and b == 0)
                    if behind:
                        shared_up(b - 1, 1 - par)
                    x_T(b + 1, 1 - par)
                    if behind:
                        shared_down(b - 1)

                def last():
                    proj(NB - 1, 1)
                    if L == 1:
                        shared_up(NB - 2, 0)
                        shared_down(NB - 2)
                x_T(0, 0)
                in_pairs(pe, stage, lambda b, par: None, last)
                KT = CHOICES[L] * NT
                pe.wait_ge(s["onehot_ready"], 1)
                pe.matmul(ps[:, 0, 0:KT * E], upb[:, :], ohb[:, 0:KT, :].rearrange("p n e -> p (n e)"),
                          start=True, stop=True)
                pe.matmul(ps[:, 1, 0:KT * E], oneb[:, :], ohb[:, 0:KT, :].rearrange("p n e -> p (n e)"),
                          start=True, stop=True).then_inc(s["counts_ready"], 1)
                if L == 1:
                    shared_up(NB - 1, 1)
                    shared_down(NB - 1)
                    pe.wait_ge(s["sh_saved"], NB)

                n_steps, n_items = len(STEPS[L]), ITEMS[L]

                def first_pass(b, g, n):
                    if n == 0:
                        pe.wait_ge(s[f"ld{g}"], BASE[L] // 2 * 3 + 48 * b + 48)
                    if L == 0:
                        wait(pe, s["s_used"], n_items * (4 * b + g) + n - 3)
                        h, qt = n // TB, n % TB
                        mm = pe.matmul(ps[:, 2 + n % 4, 0:(qt + 1) * P], Qs[:, g, h, qt * P:(qt + 1) * P],
                                       Ks[:, g, h, 0:(qt + 1) * P], start=True, stop=True)
                    else:
                        wait(pe, s["s_used"], n_items * (4 * b + g) + n - 1)
                        for qt in (n % 2 * 2, n % 2 * 2 + 1):
                            mm = pe.matmul(ps[:, 2 + qt, :], Qs[:, g, n // 2, qt * P:(qt + 1) * P],
                                           Ks[:, g, n // 2, :], start=True, stop=True)
                    mm.then_inc(s["s_ready"], 1)

                def m_T(b, g):
                    pe.wait_ge(s["s_used"], n_items * (4 * b + g) + n_items)
                    wait(pe, s["norm_done"], 4 * b + g - 2)
                    pe.transpose(ps[0:G * TB, 7, 0:P], mx[:, g].rearrange("p h q -> p (h q)"), idb
                                 ).then_inc(s["mT_ready"], 1)

                def o_T(b, g, ahead):
                    pe.wait_ge(s["o_copied"], 4 * b + g + 1)
                    if ahead:
                        pe.wait_ge(s["ml_ready"], NB * NG * L + 4 * b + g + 1 + ahead)
                    if ahead < 2:
                        pe.wait_ge(s["norm_done"], 4 * b + g)
                    for n in range(TB):
                        mm = pe.transpose(ps[:, 7, n * P:(n + 1) * P], oc[:, n * P:(n + 1) * P], idb)
                    mm.then_inc(s["oT_done"], 1)

                def weighted_v(b, g, kt):
                    t = 4 * b + g
                    upto = max(i for i, (k, _) in enumerate(STEPS[L]) if k == kt) + 1
                    pe.wait_ge(s["exp_done"], n_steps * t + upto)
                    if kt == 0:
                        pe.wait_ge(s["v_ready"], t + 1)
                        wait(pe, s["o_copied"], t)
                    q0 = first_query(L, kt)
                    for h in range(G):
                        mm = pe.matmul(ps[h * VW:(h + 1) * VW, 6, q0:], Vs[:, g, kt, h, :], PT[:, kt % 2, h, q0:],
                                       start=(kt == 0), stop=(kt == TB - 1), skip_group_check=True)
                    mm.then_inc(s["pv_done"], 1)

                def prev(b, g):
                    return (b, g - 1) if g else (b - 1, NG - 1)

                def turn_o(b):
                    pe.wait_ge(s["norm_done"], NG * (b + 1))
                    pe.wait_ge(s["s_used"], n_items * NG * NB)
                    wait(pe, s["oT2_ready"], b - 1)
                    for n in range(TB):
                        mm = pe.transpose(ps[:, 2 + b % 2, n * P:(n + 1) * P], o_sb[:, b * TB + n, :], idb)
                    mm.then_inc(s["oT2_psum"], 1)

                def project_o(b):
                    pe.wait_ge(s["oT2_ready"], b + 1)
                    wait(pe, s["sg_ready"], b - 1)
                    for n in range(TB):
                        mm = pe.matmul(ps[:, 4 + b % 2, n * P:(n + 1) * P], oT[b % 2][:, n * P:(n + 1) * P],
                                       w0[:, 5 * P:6 * P], start=True, stop=True)
                    mm.then_inc(s["s_psum"], 1)

                def attention(b0):
                    def batch(b):
                        for g in range(NG):
                            t = 4 * b + g
                            first = isinstance(b, int) and b == b0 and g == 0
                            final = isinstance(b, int) and b == NB - 1
                            last = final and g == NG - 1
                            for i, (kt, hs) in enumerate(STEPS[L]):
                                if i == 0:
                                    pe.wait_ge(s[f"min{g}"], BASE[L] + 32 * b + 32)
                                wait(pe, s["exp_done"], n_steps * t + i - 1)
                                q0 = first_query(L, kt)
                                for k, h in enumerate(hs):
                                    bank, c0 = (n_steps * g + i) % 2, k * (512 - q0)
                                    mm = pe.matmul(ps[:, bank, c0:c0 + 512 - q0],
                                                   Ks[:, g, h, kt * P:(kt + 1) * P], Qs[:, g, h, q0:],
                                                   start=True, stop=(L == 1), skip_group_check=True)
                                    if L == 0:
                                        mm = pe.matmul(ps[:, bank, c0:c0 + P], idbf[:, :], maskb[:, :],
                                                       start=False, stop=True, skip_group_check=True)
                                mm.then_inc(s["st_ready"], 1)
                                if not (final and g >= 2):
                                    for n in range(i * n_items // n_steps, (i + 1) * n_items // n_steps):
                                        first_pass(b + (g + 2) // NG, (g + 2) % NG, n)
                                if i in SUMS[L]:
                                    k, before = SUMS[L][i]
                                    if not before:
                                        weighted_v(b, g, k)
                                    elif not first:
                                        weighted_v(*prev(b, g), k)
                                if i == M_TURN[L] and not last:
                                    m_T(b + (g + 1) // NG, (g + 1) % NG)
                                if i == O_TURN[L] and not first:
                                    o_T(*prev(b, g), 0 if last else 2)
                                if L == 0 and isinstance(b, int) and b == NB - 1 and g >= 2:
                                    for k, at in enumerate(GATE[L]):
                                        if i == at - 4:
                                            turn_o((g - 2) * len(GATE[L]) + k)
                                        if i == at - 2:
                                            project_o((g - 2) * len(GATE[L]) + k)
                    batch(b0)
                    with pe.Fori(b0 + 1, b0 + HALF - 1) as b:
                        batch(b)
                    b = b0 + HALF - 1
                    batch(b)
                    for k, before in SUMS[L].values():
                        if before:
                            weighted_v(b, NG - 1, k)
                    n = 2 * len(GATE[L])
                    if L == 0 and b0:
                        turn_o(n)
                    o_T(b, NG - 1, 0 if b0 else 1)
                    if L == 0 and b0:
                        for b in range(n, NB):
                            if b + 1 < NB:
                                turn_o(b + 1)
                            project_o(b)
                pe.wait_ge(s["v_saved"], NB)
                for g in (0, 1):
                    for n in range(n_items):
                        first_pass(0, g, n)
                    if g == 0:
                        m_T(0, 0)
                attention(0)

                def turn(j, par):
                    pe.wait_ge(s[f"xe{par}"], 16 * (j // 2 + 1) if isinstance(j, int) else 16 * (half[0] + 1))
                    wait(pe, s["xeT_ready"], j - 1)
                    for n in range(UT):
                        mm = pe.transpose(ps[:, par, n * P:(n + 1) * P], xe[:, par, n, :], idb)
                    mm.then_inc(s["xeT_psum"], 1)

                def up(j, par):
                    pe.wait_ge(s["xeT_ready"], j + 1)
                    pe.wait_ge(s[f"wu{par}"], 16 * (j // 2 + 1) if isinstance(j, int) else 16 * (half[0] + 1))
                    wait(pe, s["hb_ready"], j - 1)
                    for c in range(FC):
                        mm = pe.matmul(ps[:, 2 + 2 * par + c // 2, c % 2 * U:(c % 2 + 1) * U],
                                       we[:, par, W_1 + c * P:W_1 + (c + 1) * P], xeT[:, par, :], start=True, stop=True)
                    mm.then_inc(s["h_psum"], 1)

                def down(j, par):
                    pe.wait_ge(s["h_ready"], j + 1)
                    pe.wait_ge(s[f"wd{par}"], 16 * (j // 2 + 1) if isinstance(j, int) else 16 * (half[0] + 1))
                    wait(pe, s["ye_ready"], j - 1)
                    for n in range(UT):
                        for c in range(FC):
                            mm = pe.matmul(ps[:, 6 + par, n * P:(n + 1) * P], hT[:, par, c, n * P:(n + 1) * P],
                                           we[:, par, W_2 + c * P:W_2 + (c + 1) * P], start=(c == 0), stop=(c == FC - 1))
                    mm.then_inc(s["mm2_done"], 1)
                half = [0]
                pe.wait_ge(s["norm_done"], HALF * NG)
                turn(0, 0)
                turn(1, 1)
                up(0, 0)

                def step(jj):
                    half[0] = jj + 1
                    turn(jj * 2 + 2, 0)
                    half[0] = jj
                    up(jj * 2 + 1, 1)
                    down(jj * 2, 0)
                    half[0] = jj + 1
                    turn(jj * 2 + 3, 1)
                    up(jj * 2 + 2, 0)
                    half[0] = jj
                    down(jj * 2 + 1, 1)
                each(pe, UNITS[L] // 2 - 1, step)
                n = UNITS[L] - 1
                turn(n, 0)
                up(n - 1, 1)
                down(n - 2, 0)
                up(n, 0)
                down(n - 1, 1)
                down(n, 0)
                pe.wait_ge(s["ye_ready"], UNITS[L])
                attention(HALF)

        @block.vector
        def _(dve):
            def stats(n):
                dve.bn_stats(st6[:, n, :], x_sb[:, n, :]).then_inc(s_stat, 1)

            def aggregate(n):
                return dve.bn_aggr(mv[:, n, :], st6[:, n, :])

            def statistics(at, first):
                for n in at:
                    stats(n)
                dve.wait_ge(s_stat, first + len(at))
                for n in at:
                    ins = aggregate(n)
                ins.then_inc(s_stats, 1)
            dve.wait_ge(s_x, 16)
            statistics(range(0, 8), 0)
            dve.wait_ge(s_load, 16 * 2)
            for L in (0, 1):
                s = S[L]
                chained = [0]

                def chain(ins):
                    chained[0] += 1
                    ins.then_inc(s["chain_v"], 1)
                    dve.wait_ge(s["chain_v"], chained[0])

                if L == 0:
                    chain(dve.tensor_copy(upb[:, :], cst[:, C_UP:C_UP + P]))
                    chain(dve.tensor_copy(oneb[:, :], cst[:, C_ONE:C_ONE + P]))
                    chain(dve.tensor_copy(idbf[:, :], idb))
                    chain(dve.tensor_copy(maskb[:, :], cst[:, C_MASKT:C_MASKT + P]))

                def norm(b, par):
                    bs = bass.ds(b * TB, TB)
                    wait(dve, s["xT_psum"], b - 1)
                    copies = 2 if L == 0 else 1
                    wait(dve, s[f"xn_saved{par}"], copies * 8 * (b - par))
                    dve.tensor_tensor(xns[par], x_sb[:, bs, :], mv[:, bs, 0].unsqueeze(2).broadcast_to([P, TB, P]),
                                      ALU.subtract).then_inc(s["xm_ready"], 1)
                    dve.wait_ge(s["xm_ready"], b + 1)
                    dve.tensor_tensor(xns[par], xns[par], rstd[:, 0, bs].unsqueeze(2).broadcast_to([P, TB, P]),
                                      ALU.mult).then_inc(s["xn_ready"], 1)
                    if L == 0:
                        dve.wait_ge(s["xn_ready"], b + 1)
                        dve.tensor_tensor(xn2s[par], xns[par], rstd[:, 1, bs].unsqueeze(2).broadcast_to([P, TB, P]),
                                          ALU.mult).then_inc(s["xn2_ready"], 1)

                def products(b, par):
                    if L == 0:
                        for i in (0, 1):
                            dve.wait_ge(s[f"mm_q{i}"], b + 1)
                            wait(dve, s[f"qf_{i}"], b - 1)
                            dve.tensor_tensor(cosq[par][:, i, :], ps[:, 2 * i, :], rope[:, 0, :], ALU.mult)
                            dve.tensor_tensor(sinq[par][:, i, :], ps[:, 2 * i + 1, :], rope[:, 1, :], ALU.mult
                                              ).then_inc(s[f"rope_q{i}"], 1)
                    else:
                        dve.wait_ge(s["mm_v"], b + 1)
                        bk = w1[:, 3 * P + E + 2 * F + 2:3 * P + E + 2 * F + 2 + P].unsqueeze(1).broadcast_to([P, TB, P])
                        dve.tensor_tensor(v_sb[:, bass.ds(b * TB, TB), :], ps[:, 4, :].rearrange("p (a c) -> p a c", a=TB),
                                          bk, ALU.add).then_inc(s["v_saved"], 1)
                    dve.wait_ge(s["mm_lg"], b + 1)
                    dve.tensor_copy(lg[:, bass.ds(b * TB, TB), :], ps[:, 5, 0:TB * E].rearrange("p (a e) -> p a e", a=TB)
                                    ).then_inc(s["lg_saved"], 1)

                def remainder(b, par):
                    for i in (0, 1):
                        dve.wait_ge(s[f"p1_{i}"], b + 1)
                        wait(dve, s[f"p3_{i}"], b - 1)
                        dve.tensor_tensor(r1[par][:, i, :], qf[par][:, i, :], parts[par][0][:, i, :], ALU.subtract
                                          ).then_inc(s[f"r1_{i}"], 1)

                def shared(b):
                    dve.wait_ge(s["sh_y"], b + 1)
                    sbo = w1[:, 3 * P + E + 2 * F + 2 + P + FC:3 * P + E + 2 * F + 2 + P + FC + P].unsqueeze(1).broadcast_to([P, TB, P])
                    dve.tensor_tensor(xn_sb[:, bass.ds(b * TB, TB), :], ps[:, shared_banks(b)[2], :].rearrange("p (a c) -> p a c", a=TB),
                                      sbo, ALU.add).then_inc(s["sh_saved"], 1)

                def stage(b, par):
                    if isinstance(b, int) and b == 1:
                        if L == 0:
                            chain(dve.memset(Ks[64:P].rearrange("p g h t -> p (g h t)").bitcast(F32), 0.0))
                        dve.wait_ge(s_rstd, 2 if L == 0 else 7)
                    norm(b + 1, 1 - par)
                    if L == 0 and isinstance(b, int) and b == 2:
                        dve.wait_ge(s_rstd, 3)
                    products(b, par)

                def second(b, par):
                    remainder(b, par)
                    if L == 1 and not (isinstance(b, int) and b >= NB - 2):
                        shared(b)
                if L == 0:
                    chain(dve.memset(Ks[0:64].rearrange("p g h t -> p (g h t)").bitcast(F32), neg1))
                dve.wait_ge(s_rstd, 1 + 3 * L)
                norm(0, 0)
                if L == 0:
                    dve.wait_ge(s_rest, 16 * 4)
                    statistics(range(8, NT), 8)
                in_pairs(dve, stage, second, lambda: products(NB - 1, 1))

                K = CHOICES[L]
                KT = K * NT
                dve.wait_ge(s["lg_saved"], NB)
                for par in (0, 1):
                    dve.wait_ge(s[f"xn_saved{par}"], 16 * NB // 2 * (2 if L == 0 else 1))

                def v3(k, n=KT):
                    return big[:, k, 0:n * E].rearrange("p (n e) -> p n e", e=E)

                def bc(ap, n):
                    return ap.unsqueeze(2).broadcast_to([P, n, E])
                desc = cst[:, C_DESC:C_DESC + E].unsqueeze(1).broadcast_to([P, NT, E])
                src = lg[:, :, :]
                for k in range(K):
                    top = small[:, k, 0:NT]
                    chain(dve.tensor_reduce(top, src, AX.X, ALU.max))
                    chain(dve.tensor_tensor(v3(0, NT), src, bc(top, NT), ALU.is_equal))
                    chain(dve.tensor_tensor(v3(0, NT), v3(0, NT), desc, ALU.mult))
                    chain(dve.tensor_reduce(small[:, 2, 0:NT], v3(0, NT), AX.X, ALU.max))
                    chain(dve.tensor_tensor(ohb[:, k * NT:(k + 1) * NT, :], desc, bc(small[:, 2, 0:NT], NT), ALU.is_equal))
                    if k + 1 < K:
                        chain(dve.tensor_scalar(v3(1, NT), ohb[:, 0:NT, :], -BIG, None, ALU.mult))
                        chain(dve.tensor_tensor(v3(3, NT), lg[:, :, :], v3(1, NT), ALU.add))
                        src = v3(3, NT)
                dve.sem_inc(s["onehot_ready"], 1)
                words = big[:, :, :].rearrange("p k t -> p (k t)")
                pad = NT * E

                def sums(k, back=0):
                    at = 1024 * k + pad - E * back
                    return words[:, at:at + KT * E].rearrange("p (n e) -> p n e", e=E)
                chain(dve.memset(big[:, 0:3:2, 0:pad], 0.0))
                dve.wait_ge(s["counts_ready"], 1)
                cnt = ps[:, 1, 0:KT * E].rearrange("p (n e) -> p n e", e=E)
                rank = ps[:, 0, 0:KT * E].rearrange("p (n e) -> p n e", e=E)
                chain(dve.tensor_copy(sums(0), cnt))
                a, d = 0, 1
                while d < KT:
                    chain(dve.tensor_tensor(sums(1 - a), sums(a), sums(a, d), ALU.add))
                    a, d = 1 - a, 2 * d
                total = sums(a)[:, KT - 1, :]
                tile_of = big[:, 3, 0:E * UE].rearrange("p (e j) -> p e j", e=E)
                chain(dve.tensor_tensor(tile_of, total.unsqueeze(2).broadcast_to([P, E, UE]),
                                        cst[:, C_JU:C_JU + UE].unsqueeze(1).broadcast_to([P, E, UE]), ALU.is_gt))
                chain(dve.tensor_reduce(small[:, 4, 0:E], tile_of, AX.X, ALU.add))
                chain(dve.tensor_copy(small[:, 5, 0:E], small[:, 4, 0:E]))
                c, d = 5, 1
                while d < E:
                    chain(dve.tensor_copy(small[:, 11 - c, 0:d], small[:, c, 0:d]))
                    chain(dve.tensor_tensor(small[:, 11 - c, d:E], small[:, c, d:E], small[:, c, 0:E - d], ALU.add))
                    c, d = 11 - c, 2 * d
                nj = UNITS[L]
                te = big[:, 3, 0:nj * E].rearrange("p (j e) -> p j e", e=E)
                chain(dve.tensor_tensor(te, cst[:, C_J:C_J + nj].unsqueeze(2).broadcast_to([P, nj, E]),
                                        small[:, c, 0:E].unsqueeze(1).broadcast_to([P, nj, E]), ALU.is_ge))
                chain(dve.tensor_reduce(small[:, 7, 0:nj], te, AX.X, ALU.add))
                chain(dve.tensor_scalar(tex[:, 0:nj], small[:, 7, 0:nj], float(E - 1), None, ALU.min))
                dve.sem_inc(s["tiles_ready"], 1)
                chain(dve.tensor_tensor(small[:, 11 - c, 0:E], small[:, c, 0:E], small[:, 4, 0:E], ALU.subtract))
                chain(dve.tensor_scalar(small[:, 11 - c, 0:E], small[:, 11 - c, 0:E], float(U), None, ALU.mult))
                row = sums(a)
                chain(dve.tensor_tensor(row, row, rank, ALU.add))
                chain(dve.tensor_tensor(row, row, small[:, 11 - c, 0:E].unsqueeze(1).broadcast_to([P, KT, E]), ALU.add))
                chain(dve.tensor_tensor(row, row, ohb[:, 0:KT, :], ALU.mult))
                chain(dve.tensor_reduce(small[:, 7, 0:KT], row, AX.X, ALU.add))
                dve.tensor_copy(pos[:, 0:KT], small[:, 7, 0:KT]).then_inc(s["pos_ready"], 1)
                if L == 1:
                    shared(NB - 2)
                    shared(NB - 1)

                n_steps, n_items = len(STEPS[L]), ITEMS[L]

                def row_max(b, g, n):
                    at = n_items * (4 * b + g) + n + 1
                    if L == 0:
                        wait_apart(dve, s["s_ready"], at, passed_dve)
                        h, qt = n // TB, n % TB
                        N = (qt + 1) * P
                        dve.tensor_tensor_reduce(dump[:, P * qt * (qt + 1) // 2:P * (qt + 1) * (qt + 2) // 2], ps[:, 2 + n % 4, 0:N],
                                                 cst[:, C_MASK + 512 - N:C_MASK + 512], 1.0, -3.0e38, ALU.add, ALU.max,
                                                 mx[:, g, h, qt:qt + 1]).then_inc(s["s_used"], 1)
                    else:
                        dve.wait_ge(s["s_ready"], at)
                        qt = n % 2 * 2
                        dve.tensor_reduce(mx[:, g, n // 2, qt:qt + 2], ps[:, 2 + qt:4 + qt, :], AX.X, ALU.max
                                          ).then_inc(s["s_used"], 1)

                def m_lo(b, g):
                    dve.wait_ge(s["mh_ready"], NB * NG * L + 4 * b + g + 1)
                    wait(dve, s[f"min{g}"], BASE[L] + 32 * b)
                    dve.tensor_tensor(mlo[:, g, :], ps[0:G * TB, 7, 0:P], mhi[:, g, :], ALU.subtract
                                      ).then_inc(s["ml_ready"], 1)

                def normalize(b, g):
                    t = 4 * b + g
                    dve.wait_ge(s["oT_done"], t + 1)
                    oT4 = ps[:, 7, :].rearrange("p (q h w) -> p q h w", q=TB, h=G)
                    dve.reciprocal(rec[:, :, :], oT4[:, :, :, DH]).then_inc(s["rec_ready"], 1)
                    dve.wait_ge(s["rec_ready"], t + 1)
                    dst = o_sb[:, bass.ds(b * TB, TB), g * G * DH:(g + 1) * G * DH].rearrange("p q (h d) -> p q h d", h=G)
                    dve.tensor_tensor(dst, oT4[:, :, :, 0:DH], rec[:, :, :].unsqueeze(3).broadcast_to([P, TB, G, DH]),
                                      ALU.mult).then_inc(s["norm_done"], 1)

                def prev(b, g):
                    return (b, g - 1) if g else (b - 1, NG - 1)

                def gate(b):
                    at = slice(b * TB, (b + 1) * TB)
                    dve.wait_ge(s["silu_ready"], b // 2 + 1)
                    if L == 0:
                        dve.wait_ge(s["s_psum"], b + 1)
                    sv = ps[:, 4 + b % 2, :].rearrange("p (a c) -> p a c", a=TB) if L == 0 else o_sb[:, at, :]
                    dve.tensor_tensor(yg_sb[:, at, :], yg_sb[:, at, :], sv, ALU.mult).then_inc(s["sg_ready"], 1)
                    if L == 1:
                        dve.wait_ge(s["sg_ready"], b + 1)
                        dve.tensor_tensor(x_sb[:, at, :], x_sb[:, at, :], yg_sb[:, at, :], ALU.add).then_inc(s["x_ready"], 1)
                    elif b:
                        new_statistics(b - 1)

                def new_statistics(b):
                    dve.wait_ge(s["x_ready"], b + 1)
                    statistics(range(b * TB, (b + 1) * TB), NT + b * TB)

                def attention(b0):
                    def batch(b):
                        for g in range(NG):
                            first = isinstance(b, int) and b == b0 and g == 0
                            final = isinstance(b, int) and b == NB - 1
                            for i in range(n_steps):
                                if not (final and g >= 2):
                                    for n in range(i * n_items // n_steps, (i + 1) * n_items // n_steps):
                                        row_max(b + (g + 2) // NG, (g + 2) % NG, n)
                                if i == M_SPLIT[L] and not (final and g == NG - 1):
                                    m_lo(b + (g + 1) // NG, (g + 1) % NG)
                                if i == O_NORM[L] and not first:
                                    normalize(*prev(b, g))
                                if isinstance(b, int) and b == NB - 1 and g >= 2 and i in GATE[L]:
                                    gate((g - 2) * len(GATE[L]) + GATE[L].index(i))
                    batch(b0)
                    with dve.Fori(b0 + 1, b0 + HALF - 1) as b:
                        batch(b)
                    batch(b0 + HALF - 1)
                    normalize(b0 + HALF - 1, NG - 1)
                for g in (0, 1):
                    for n in range(n_items):
                        row_max(0, g, n)
                        if g == 1 and n == 1:
                            m_lo(0, 0)
                attention(0)

                def head(j, par):
                    dve.wait_ge(s["xeT_psum"], j + 1)
                    wait(dve, s["h_psum"], j - 1)
                    if L == 0:
                        wait_apart(dve, s[f"wu{par}"], 16 * (j // 2 + 1) if isinstance(j, int) else 16 * (half[0] + 1), passed_dve)
                        dve.tensor_scalar(xeT[:, par, :], ps[:, par, 0:U], we[:, par, W_G:W_G + 1],
                                          we[:, par, W_LB:W_LB + 1], ALU.mult, ALU.add).then_inc(s["xeT_ready"], 1)
                    else:
                        dve.tensor_copy(xeT[:, par, :], ps[:, par, 0:U]).then_inc(s["xeT_ready"], 1)

                def bias1(j, par):
                    dve.wait_ge(s["h_psum"], j + 1)
                    wait(dve, s["h_ready"], j - 1)
                    dve.tensor_tensor(hb[:, par], ps[:, 2 + 2 * par:4 + 2 * par, :].rearrange("p a (c t) -> p (a c) t", c=2),
                                      we[:, par, W_B1:W_B1 + FC].unsqueeze(2).broadcast_to([P, FC, U]), ALU.add
                                      ).then_inc(s["hb_ready"], 1)

                def bias2(j, par):
                    dve.wait_ge(s["mm2_done"], j + 1)
                    wait(dve, s[f"yo{par}"], 16 * (j // 2) if isinstance(j, int) else 16 * half[0])
                    dve.tensor_tensor(ye[:, par], ps[:, 6 + par, 0:U].rearrange("p (n d) -> p n d", n=UT),
                                      we[:, par, W_B2:W_B2 + P].unsqueeze(1).broadcast_to([P, UT, P]), ALU.add
                                      ).then_inc(s["ye_ready"], 1)
                if L == 1:
                    chain(dve.tensor_tensor(lg[:, :, :], lg[:, :, :], bc(small[:, 0, 0:NT], NT), ALU.subtract))
                    dve.sem_inc(s["gate_exp"], 1)
                    chain(dve.tensor_tensor(small[:, 2, 0:NT], small[:, 1, 0:NT], small[:, 0, 0:NT], ALU.subtract))
                    dve.wait_ge(s["gate_exp"], 2)
                    dve.sem_inc(s["gate_exp"], 1)
                    chain(dve.tensor_reduce(small[:, 3, 0:NT], lg[:, :, :], AX.X, ALU.add))
                    dve.wait_ge(s["gate_exp"], 4)
                    chain(dve.reciprocal(wch[:, 0, :], small[:, 3, 0:NT]))
                    chain(dve.tensor_tensor(wch[:, 1, :], small[:, 2, 0:NT], wch[:, 0, :], ALU.mult))
                half = [0]
                head(0, 0)
                head(1, 1)
                bias1(0, 0)

                def step(jj):
                    bias1(jj * 2 + 1, 1)
                    half[0] = jj + 1
                    head(jj * 2 + 2, 0)
                    half[0] = jj
                    bias2(jj * 2, 0)
                    bias1(jj * 2 + 2, 0)
                    half[0] = jj + 1
                    head(jj * 2 + 3, 1)
                    half[0] = jj
                    bias2(jj * 2 + 1, 1)
                each(dve, UNITS[L] // 2 - 1, step)
                n = UNITS[L] - 1
                bias1(n - 1, 1)
                head(n, 0)
                bias2(n - 2, 0)
                bias1(n, 0)
                bias2(n - 1, 1)
                bias2(n, 0)

                attention(HALF)
                for b in range(2 * len(GATE[L]), NB):
                    gate(b)
                if L == 0:
                    new_statistics(NB - 1)
                if L == 0:
                    dve.wait_ge(s_w1, 16)


_INS = ["x", "rope", "const", "w0", "w1", "e0", "e1"]
_OUTS = [((8, 512, 128), 'float32')]


def layout(np, i):
    a = {k: np.asarray(v) for k, v in i.items()}
    f32 = np.float32
    r = np.arange(P)
    order = (r % H) * DH + r // H
    swapped = (r % H) * DH + ((r // H) ^ 1)
    wq, wk = a["L0_attn_wq"], a["L0_attn_wk"]
    w0 = np.concatenate([wq[order].T, wq[swapped].T, wk[order].T, wk[swapped].T, a["L0_attn_wv"].T, a["L0_attn_wo"].T,
                         a["L0_ffn_centroids"].T], axis=1)
    chunks = lambda w: w.reshape(FC, P, P).transpose(1, 0, 2).reshape(P, F)
    everywhere = lambda v: np.broadcast_to(v[None, :], (P, P))
    w1 = np.concatenate([a["L1_attn_Wq"][:, order], a["L1_attn_Wk"][:, order], a["L1_attn_Wk"], a["L1_ffn_gate_w"].T,
                         a["L1_ffn_sw_in"], chunks(a["L1_ffn_sw_out"]), a["L1_attn_bq"][order][:, None],
                         a["L1_attn_bk"][order][:, None], everywhere(a["L1_attn_bk"]),
                         a["L1_ffn_sb_in"].reshape(FC, P).T, everywhere(a["L1_ffn_sb_out"])], axis=1)

    def experts(W1, W2, b1, b2, *more):
        return np.ascontiguousarray(np.stack([np.concatenate(
            [chunks(W2[e]), everywhere(b2[e]), W1[e], b1[e].reshape(FC, P).T] + [m[e][:, None] for m in more], axis=1)
            for e in range(E)]))
    e0 = experts(a["L0_ffn_W1"], a["L0_ffn_W2"], a["L0_ffn_b1"], a["L0_ffn_b2"], a["L0_ffn_ln_g"], a["L0_ffn_ln_b"])
    e1 = experts(a["L1_ffn_w_in"], a["L1_ffn_w_out"], a["L1_ffn_b_in"], a["L1_ffn_b_out"])
    d = r // H
    freq = (f32(1.0) / f32(10000.0) ** (np.arange(0, DH, 2, dtype=f32) / f32(DH))).astype(f32)
    ang = np.outer(freq[d // 2], np.arange(TB * P, dtype=f32)).astype(f32)
    rope = np.stack([np.cos(ang), np.where(d % 2 == 0, -1, 1)[:, None] * np.sin(ang)], axis=1).astype(f32)
    const = np.zeros((P, NCONST), f32)
    const[:, C_ID:C_ID + P] = np.eye(P)
    const[:, C_UP:C_UP + P] = (r[:, None] < r[None, :]) - 1.0
    const[:, C_ONE:C_ONE + P] = 1
    const[:, C_MASK + 384:C_MASK + 512] = np.where(r[None, :] > r[:, None], -BIG, 0)
    const[:, C_MASKT:C_MASKT + P] = np.where(r[:, None] > r[None, :], -BIG, 0)
    const[:, C_DESC:C_DESC + E] = E - np.arange(E)
    const[:, C_JU:C_JU + UE] = U * np.arange(UE)
    const[:, C_J:C_J + UNITS[1]] = np.arange(UNITS[1])
    const[:, C_NHALF:C_NHALF + NT] = -0.5
    return [a["L0_attn_x"], rope, const, w0, w1, e0, e1]


def kernel(**inputs):
    import numpy as _np
    import concourse.bacc as _bacc
    from concourse import mybir as _mybir
    from concourse.bass_utils import run_bass_kernel_spmd as _run

    nc = _bacc.Bacc("TRN2", target_bir_lowering=False, num_devices=1)
    arrays, args = {}, []
    for name, a in zip(_INS, layout(_np, inputs)):
        a = _np.ascontiguousarray(a)
        arrays[f"in_{name}_dram"] = a
        args.append(nc.dram_tensor(f"in_{name}_dram", a.shape, _mybir.dt.from_np(a.dtype), kind="ExternalInput").ap())
    for i, (shape, dtype) in enumerate(_OUTS):
        dt = _mybir.dt.from_np(_np.dtype(dtype))
        args.append(nc.dram_tensor(f"out_{i}_dram", shape, dt, kind="ExternalOutput").ap())
    build(nc, *args)
    r = _run(nc, [arrays], core_ids=[0])
    got = tuple(r.results[0][f"out_{i}_dram"] for i in range(len(_OUTS)))
    return got[0]
```
